# Optimizing a Trainium2 kernel written in Bass

```python
import numpy as np
import jax
import jax.numpy as jnp

def _softmax(x, axis=-1):
    return jax.nn.softmax(x, axis=axis)
def _gelu(x):
    return jax.nn.gelu(x, approximate=True)
def _silu(x):
    return jax.nn.silu(x)
def _sigmoid(x):
    return jax.nn.sigmoid(x)
def _layernorm(x, axis=-1, eps=1e-5):
    m = jnp.mean(x, axis=axis, keepdims=True)
    v = jnp.var(x, axis=axis, keepdims=True)
    return (x - m) / jnp.sqrt(v + eps)
def _scatter_add(tgt, idx, src, axis=0):
    return tgt.at[idx].add(src)
def _segment_sum(src, seg, n):
    return jax.ops.segment_sum(src, seg, n)

kernel_name = 'mk_conv_seq_d1_conv_nchw256_150d15'

def setup_inputs(seed: int = 0):
    np.random.seed(seed)
    _w = jnp.asarray
    def _rec_inputs():
        import jax
        import jax.numpy as jnp
        _gk = jax.random.key(seed)
        x = -7.109e-05 + 0.9999 * jax.random.normal(jax.random.fold_in(_gk, 1), (4, 256, 256, 256), jnp.float32)
        return x
    x = _rec_inputs()
    def _L0_conv_setup():
        import jax, jax.numpy as jnp
        from jax import lax
        import numpy as np
        K = 3

        def _hamming2d():
            return jnp.asarray(np.outer(np.hamming(K), np.hamming(K)), dtype=jnp.float32)
        key = jax.random.key(seed)
        k1, k2, k3 = jax.random.split(key, 3)
        B, C, H, W = (4, 256, 256, 256)
        comp = 64
        x = jax.random.normal(k1, (B, C, H, W), dtype=jnp.float32)
        w_comp = jax.random.normal(k2, (comp, C), dtype=jnp.float32) * np.sqrt(2.0 / (C + comp))
        w_gen = jax.random.normal(k3, (K * K, comp, 3, 3), dtype=jnp.float32) * 0.001
        b_gen = jnp.zeros((K * K,), dtype=jnp.float32)
        return {'x': x, 'w_comp': w_comp, 'w_gen': w_gen, 'b_gen': b_gen}
    _L0_conv_all = _L0_conv_setup()
    _L0_conv_in = {k: v for k, v in _L0_conv_all.items() if k in ('w_comp', 'w_gen', 'b_gen', )}
    del _L0_conv_all

    return {
        "x": x,
        "L0_conv_w_comp": _L0_conv_in["w_comp"],
        "L0_conv_w_gen": _L0_conv_in["w_gen"],
        "L0_conv_b_gen": _L0_conv_in["b_gen"],
    }

def reference(x, L0_conv_w_comp, L0_conv_w_gen, L0_conv_b_gen):
    import jax
    import jax.numpy as jnp
    def _L0_conv_ref(x, w_comp, w_gen, b_gen):
        import jax, jax.numpy as jnp
        from jax import lax
        import numpy as np
        K = 3

        def _hamming2d():
            return jnp.asarray(np.outer(np.hamming(K), np.hamming(K)), dtype=jnp.float32)
        B, C, H, W = x.shape
        KK = K * K
        compressed = jnp.einsum('bchw,oc->bohw', x, w_comp)
        logits = lax.conv_general_dilated(compressed, w_gen, window_strides=(1, 1), padding='SAME', dimension_numbers=('NCHW', 'OIHW', 'NCHW')) + b_gen[None, :, None, None]
        kw = jax.nn.softmax(logits, axis=1)
        kw = kw.reshape(B, H, W, K, K) * _hamming2d()
        kw = kw / (kw.sum(axis=(-1, -2), keepdims=True) + 1e-08)
        kw = jnp.transpose(kw, (0, 3, 4, 1, 2)).reshape(B, KK, H, W)
        pad = K // 2
        xp = jnp.pad(x, ((0, 0), (0, 0), (pad, pad), (pad, pad)), mode='reflect')
        agg = jnp.zeros_like(x)
        for i in range(K):
            for j in range(K):
                agg = agg + xp[:, :, i:i + H, j:j + W] * kw[:, i * K + j][:, None]
        highpass = x - agg
        return x + highpass

    def _gn(v, G=32, eps=1e-5):
        B_, C_, H_, W_ = v.shape
        g = v.reshape(B_, G, C_ // G, H_, W_)
        m = jnp.mean(g, axis=(2, 3, 4), keepdims=True)
        s = jnp.var(g, axis=(2, 3, 4), keepdims=True)
        return ((g - m) / jnp.sqrt(s + eps)).reshape(v.shape)

    def _ln_c(v, eps=1e-6):
        m = jnp.mean(v, axis=1, keepdims=True)
        s = jnp.var(v, axis=1, keepdims=True)
        return (v - m) / jnp.sqrt(s + eps)

    def _ln_t(v, eps=1e-5):
        m = jnp.mean(v, axis=-1, keepdims=True)
        s = jnp.var(v, axis=-1, keepdims=True)
        return (v - m) / jnp.sqrt(s + eps)

    def _to_tokens(v):
        B_, C_, H_, W_ = v.shape
        return v.reshape(B_, C_, H_ * W_).transpose(0, 2, 1)
    def _from_tokens(t, like):
        B_, C_, H_, W_ = like.shape
        return t.transpose(0, 2, 1).reshape(B_, C_, H_, W_)

    x = _L0_conv_ref(x, L0_conv_w_comp, L0_conv_w_gen, L0_conv_b_gen)
    return x


_drawn_inputs = setup_inputs


def setup_inputs(seed=0):
    import zlib

    import numpy as np

    out = dict(_drawn_inputs(seed))
    spreads = {'L0_conv_b_gen': (0.0, 0.8)}
    factors = {'L0_conv_w_comp': 8.0, 'L0_conv_w_gen': 8.0}
    for name, (base, spread) in spreads.items():
        noise = np.random.default_rng([zlib.crc32(name.encode()), seed]).standard_normal(out[name].shape)
        drawn = base * np.exp(spread * noise) if base else spread * noise
        out[name] = jnp.asarray(drawn.astype(out[name].dtype))
    for name, factor in factors.items():
        out[name] = (out[name] * factor).astype(out[name].dtype)
    return out
```

```python
import numpy as np

import concourse.bass as bass
import concourse.mybir as mybir
from concourse.alu_op_type import AluOpType as ALU

B, C, H, W = 4, 256, 256, 256
COMP = 64
K = 3
KK = K * K
P = 128
CH = C // P
WH = W // P

TILE_ROWS = 8
SLOTS = 4
UNIT_ROWS = TILE_ROWS * SLOTS
UNITS = H // UNIT_ROWS
TILES = H // TILE_ROWS
BLOCK_ROWS = 16
BLOCKS = H // BLOCK_ROWS
JK = K * KK
TAPS = K * JK

CHUNK = 128
CHUNKS = (H // P) * (W // CHUNK)

PR, PC = 7, 12
IR, IC = PR + 2, PC + 2
PIX = PR * PC
IPIX = IR * IC
STRIPS = -(-H // PR)
TAIL_ROWS = H - (STRIPS - 1) * PR
TURN = 4
TURNS = (STRIPS - 1) // TURN
PATCHES = -(-W // PC)
LAST_COLS = W - (PATCHES - 1) * PC
PAIRS = PATCHES // 2
GROUP = 6
GROUPS = -(-PATCHES // GROUP)
KW_PITCH = PATCHES * PC
PARTS = 3

PAIR_COUNT = 408
STRIP_COUNT = STRIPS + 1
GROUP_COUNT = STRIPS * GROUPS
assert STRIPS * PAIRS + 1 == PAIR_COUNT and PAIR_COUNT % TURN == 0 and GROUP_COUNT % 2 == 0
assert TURNS * TURN + 1 == STRIPS and TURN == SLOTS and STRIP_COUNT % 2 == 0
assert 0 < TAIL_ROWS <= PR < TILE_ROWS and IPIX <= P and PIX * GROUP <= 512


NUMBERS = ["eps", "-2", "-1", "0", "2"]


def constants():
    ident = np.eye(P)
    from_left = np.eye(P, k=1)
    from_right = np.eye(P, k=-1)
    carry_left = np.zeros((P, P))
    carry_left[P - 1, 0] = 1
    carry_right = np.zeros((P, P))
    carry_right[0, P - 1] = 1
    spread = np.zeros((P, K, IPIX))
    mask = np.zeros((P, PR, PC))
    for r in range(IR):
        for s in range(IC):
            for phase in range(K):
                for part in range(PARTS):
                    spread[part * KK + (r - phase) % K * K + s % K, phase, r * IC + s] = 1
            for y in range(PR):
                for z in range(PC):
                    mask[r * IC + s, y, z] = 0 <= r - y < K and 0 <= s - z < K
    window = np.broadcast_to(np.outer(np.hamming(K), np.hamming(K)).reshape(-1), (P, KK))
    values = np.broadcast_to([1e-8 if n == "eps" else float(n) for n in NUMBERS], (P, len(NUMBERS)))
    return np.concatenate([ident, from_left, from_right, carry_left, carry_right,
                           spread.reshape(P, -1), mask.reshape(P, -1), window, values],
                          1).astype(np.float32)


def group_end(g):
    return min((g + 1) * GROUP, PATCHES) // 2


def build(nc, ctx, x, w_comp, w_gen, b_gen, const, out, images=B):
    f32, bf16 = mybir.dt.float32, mybir.dt.bfloat16
    ACT = mybir.ActivationFunctionType
    AX = mybir.AxisListType

    def sb(name, shape, dt=f32):
        return ctx.enter_context(nc.sbuf_tensor(name, shape, dt))

    def sem(name):
        return ctx.enter_context(nc.semaphore(name))

    planes = nc.dram_tensor("planes", (images, KK, H, W), f32).ap()
    coefs = nc.dram_tensor("coefs", (images, PARTS * KK, H, W), bf16).ap()
    reread = planes.rearrange("n k h w -> n (k h w)").rearrange("n (h q) -> n h q", q=W * KK)

    xs = [sb(f"x_rows{q}", [P, CH, TILE_ROWS, W]) for q in range(SLOTS)]
    patches = [sb(f"patches{j}", [P, CH, PATCHES, IPIX]) for j in range(2)]
    kw = [sb(f"kw_strip{j}", [P, PR, KW_PITCH], bf16) for j in range(2)]
    out_rows = [sb(f"out_rows{j}", [P, CH, PR, W]) for j in range(2)]
    const_sb = sb("const_sb", [P, const.shape[1]])
    spread_sb = sb("spread_sb", [P, K, IPIX], bf16)
    comp_sb = sb("comp_sb", [COMP, C])
    gen_sb = sb("gen_sb", [COMP, TAPS])
    bias_sb = sb("bias_sb", [P, KK])
    taps_sb = sb("taps_sb", [P, CH, TAPS])
    rowsum = sb("rowsum", [P, WH, UNIT_ROWS, JK])
    logits = sb("logits", [P, WH * UNIT_ROWS, KK])
    top = sb("top", [P, WH * UNIT_ROWS])
    total = sb("total", [P, WH * UNIT_ROWS])
    scale = sb("scale", [P, WH * UNIT_ROWS])
    probs = sb("probs", [P, WH, KK, UNIT_ROWS])
    map_rows = sb("map_rows", [K * UNIT_ROWS, K, W])
    turned = [sb(f"turned{j}", [P, 2, C]) for j in range(TURN)]
    band = [sb(f"band{j}", [P, GROUP, PR, PC]) for j in range(2)]
    raw = sb("raw", [P, CHUNK, KK])
    weighed = sb("weighed", [P, KK, CHUNK])
    coef = sb("coef", [P, KK, CHUNK])
    pieces = sb("pieces", [P, PARTS * KK, CHUNK], bf16)
    norm = sb("norm", [P, 4, CHUNK])
    primer = sb("primer", [P, 32])

    at = 0
    def const_part(n):
        nonlocal at
        at += n
        return const_sb[:, at - n:at]
    ident, from_left, from_right, carry_left, carry_right = (const_part(P) for _ in range(5))
    spread32 = const_part(K * IPIX)
    mask = const_part(PIX).rearrange("p (y z) -> p y z", y=PR)
    window = const_part(KK).rearrange("p (i j) -> p i j", i=K)
    numbers = const_part(len(NUMBERS))

    banks = [ctx.enter_context(nc.psum_tensor(f"bank{n}", [P, 512], f32)) for n in range(8)]
    gather_ps = [[banks[2 * par + wh] for wh in range(WH)] for par in range(2)]
    logit_ps = banks[4:6]
    map_ps = banks[6:8]
    turn_ps = banks[0:2]
    spread_ps = banks[2:4]
    blend_ps = [banks[4:6], banks[6:8]]

    const_in = sem("const_in")
    cleared = sem("cleared")
    spread_ready = sem("spread_ready")
    taps_made = sem("taps_made")
    taps_copied = sem("taps_copied")
    tile_in = [sem(f"tile_in{q}") for q in range(SLOTS)]
    scanned = sem("scanned")
    gathered = sem("gathered")
    lifted = sem("lifted")
    shifted = sem("shifted")
    logits_taken = sem("logits_taken")
    topped = sem("topped")
    centered = sem("centered")
    powered = sem("powered")
    totalled = sem("totalled")
    inverted = sem("inverted")
    probs_made = sem("probs_made")
    flipped = sem("flipped")
    mapped = sem("mapped")
    planes_stored = sem("planes_stored")
    raw_in = sem("raw_in")
    refining = sem("refining")
    coefs_stored = sem("coefs_stored")
    strip_in = [sem(f"strip_in{q}") for q in range(SLOTS)]
    kw_in = [sem(f"kw_in{j}") for j in range(2)]
    windowed = sem("windowed")
    crossed = sem("crossed")
    copied = sem("copied")
    spreaded = sem("spreaded")
    banded = sem("banded")
    blended = sem("blended")
    collected = sem("collected")
    collected_act = sem("collected_act")
    stored = [sem(f"stored{j}") for j in range(2)]

    def first_image(img):
        return isinstance(img, int) and img == 0

    def pairs(img, n):
        return (img + 1) * PAIR_COUNT + n

    def groups(img, n):
        return (img + 1) * GROUP_COUNT + n

    def act_groups(img, n):
        return (img + 1) * STRIPS * (GROUPS - 1) + n

    def strips(img, n):
        return (img + 1) * STRIP_COUNT + n

    def uses(slots, slot):
        return len(range(slot, STRIPS, slots))

    def ahead(eng, register, value):
        if isinstance(value, int):
            return value
        eng.reg_mov(register, value)
        return register

    block = ctx.enter_context(nc.Block())

    def schedule(eng, scan, blend):
        scan(0)
        if images > 1:
            with eng.Fori(0, images - 1) as n:
                scan(n + 1)
                blend(n, False)
        blend(images - 1, True)

    @block.sync
    def _(sp):
        second_wait = sp.alloc_register("second_wait")

        def load_x(q, img, row, rows, at, signal):
            src = x[bass.ds(img, 1)].rearrange("n (c p) h w -> p c (n h) w", c=CH)
            for c in range(CH):
                nc.sync.dma_start(xs[q][:, c, at:at + rows], src[:, c, bass.ds(row, rows), :]).then_inc(signal, 16)

        def scan(img):
            for q in range(SLOTS):
                if not first_image(img):
                    laid = ahead(sp, second_wait, strips(img - 2, STRIPS - (SLOTS - q) % SLOTS))
                    sp.wait_ge(scanned, img * TILES)
                    sp.wait_ge(windowed, laid)
                load_x(q, img, q * TILE_ROWS, TILE_ROWS, 0, tile_in[q])
            with sp.Fori(1, UNITS) as it:
                for q in range(SLOTS):
                    sp.wait_ge(scanned, img * TILES + (it - 1) * SLOTS + q + 1)
                    load_x(q, img, (it * SLOTS + q) * TILE_ROWS, TILE_ROWS, 0, tile_in[q])

        def load_strip(img, t, q, rows=PR):
            load_x(q, img, t * PR + 1, rows, 1, strip_in[q])

        def load_kw(img, t, j, rows=PR):
            src = coefs[bass.ds(img, 1)].rearrange("n p h w -> p (n h) w")
            nc.sync.dma_start(kw[j][0:PARTS * KK, 0:rows, 0:W],
                              src[:, bass.ds(t * PR, rows), :]).then_inc(kw_in[j], 16)

        def store_strip(img, t, slot, rows=PR):
            at = img * (C * H * W) + t * (PR * W)
            act_done = ahead(sp, second_wait, act_groups(img, (t + 1) * (GROUPS - 1)))
            dst = bass.AP(out.tensor, at, [[H * W, P], [P * H * W, CH], [1, rows * W]])
            sp.wait_ge(collected, groups(img, (t + 1) * GROUPS))
            sp.wait_ge(collected_act, act_done)
            nc.sync.dma_start(dst, out_rows[slot][:, :, 0:rows, :].rearrange(
                "p c y w -> p c (y w)")).then_inc(stored[slot], 16)

        def blend(img, last):
            for q in range(SLOTS):
                if last and images > 1:
                    sp.wait_ge(windowed, strips(img - 1, STRIPS - (SLOTS - q) % SLOTS))
                else:
                    scans = img + 1 if last else img + 2
                    sp.wait_ge(scanned, scans * TILES - SLOTS + q + 1)
                if q == 0:
                    load_x(0, img, 0, TILE_ROWS, 0, strip_in[0])
                else:
                    load_strip(img, q, q)
            spread_before = ahead(sp, second_wait, groups(img, 0))
            sp.wait_ge(coefs_stored, 16 * CHUNKS * (img + 1))
            sp.wait_ge(cleared, 1)
            sp.wait_ge(spreaded, spread_before)
            for j in range(2):
                load_kw(img, j, j)
            with sp.Fori(0, TURNS - 1) as turn:
                for q in range(TURN):
                    t = turn * TURN + q
                    sp.wait_ge(windowed, strips(img, t + 1))
                    load_strip(img, t + TURN, q)
                    sp.wait_ge(spreaded, groups(img, (t + 1) * GROUPS))
                    load_kw(img, t + 2, q % 2)
                    store_strip(img, t, q % 2)
            for q in range(TURN):
                t = (TURNS - 1) * TURN + q
                if q == 0:
                    sp.wait_ge(windowed, strips(img, t + 1))
                    src = x[bass.ds(img, 1)].rearrange("n (c p) h w -> p c (n h) w", c=CH)
                    first = (STRIPS - 1) * PR + 1
                    nc.sync.dma_start(xs[0][:, :, 1:TAIL_ROWS], src[:, :, first:H]).then_inc(strip_in[0], 16)
                    nc.sync.dma_start(xs[0][:, :, TAIL_ROWS], src[:, :, H - 2]).then_inc(strip_in[0], 16)
                if t + 2 < STRIPS:
                    sp.wait_ge(spreaded, groups(img, (t + 1) * GROUPS))
                    load_kw(img, t + 2, q % 2, PR if t + 2 < STRIPS - 1 else TAIL_ROWS)
                store_strip(img, t, q % 2)
            store_strip(img, STRIPS - 1, 0, TAIL_ROWS)

        nc.sync.dma_start(const_sb[:], const).then_inc(const_in, 16)
        nc.sync.dma_start(comp_sb[:], w_comp).then_inc(const_in, 16)
        nc.sync.dma_start(gen_sb[:], w_gen).then_inc(const_in, 16)
        nc.sync.dma_start(bias_sb[:], b_gen[0:1, :].to_broadcast((P, KK))).then_inc(const_in, 16)
        schedule(sp, scan, blend)
        for slot in range(2):
            sp.wait_ge(stored[slot], 16 * (1 + images * (STRIPS // 2 + 1 - slot)))

    @block.tensor
    def _(pe):
        def scan_row(img, rr, first_unit, it):
            q, row = divmod(rr, TILE_ROWS)
            par, yy = divmod(rr, BLOCK_ROWS)
            if row == 0:
                pe.wait_ge(tile_in[q], 32 * (img * UNITS + it + 1))
            if yy == BLOCK_ROWS - 1 and not (first_unit and par == 0):
                pe.wait_ge(lifted, img * BLOCKS + 2 * it + par)
            last = None
            for wh in range(WH):
                here, other = gather_ps[par][wh], gather_ps[1 - par][wh]
                for c in range(CH):
                    px = xs[q][:, c, row, wh * P:(wh + 1) * P]

                    def add(bank, slot, tap0, n, start=False, stop=False):
                        return nc.tensor.matmul(
                            bank[:, slot * JK:(slot + n) * JK], px,
                            taps_sb[:, c, tap0 * JK:(tap0 + n) * JK],
                            start=start, stop=stop, skip_group_check=True)

                    if yy == 0:
                        above = not (first_unit and par == 0)
                        if above:
                            done = add(other, BLOCK_ROWS - 1, 0, 1, stop=True)
                            if wh == WH - 1 and c == CH - 1:
                                done.then_inc(gathered, 1)
                        last = add(here, 0, 1, 2, start=not above and c == 0)
                    elif yy == BLOCK_ROWS - 1:
                        add(here, yy - 1, 0, 2)
                        last = add(other, 0, 2, 1, start=c == 0)
                    else:
                        last = add(here, yy - 1, 0, 3)
            if row == TILE_ROWS - 1:
                last.then_inc(scanned, 1)

        def shift(img, u):
            pe.wait_ge(lifted, img * BLOCKS + 2 * u + 2)
            pe.wait_ge(logits_taken, 2 * (img * UNITS + u) + 1)
            for wh in range(WH):
                o = logit_ps[wh][:, 0:UNIT_ROWS * KK]

                def tap(j, half):
                    return rowsum[:, half, :, j * KK:(j + 1) * KK]
                nc.tensor.matmul(o, from_left, tap(0, wh), start=True, stop=False)
                nc.tensor.matmul(o, ident, tap(1, wh), start=False, stop=False)
                nc.tensor.matmul(o, from_right, tap(2, wh), start=False, stop=False)
                if wh == 0:
                    last = nc.tensor.matmul(o, carry_right, tap(2, 1), start=False, stop=True)
                else:
                    last = nc.tensor.matmul(o, carry_left, tap(0, 0), start=False, stop=True)
            last.then_inc(shifted, 1)

        def flip(img, u):
            pe.wait_ge(probs_made, img * UNITS + u + 1)
            pe.wait_ge(mapped, 2 * (img * UNITS + u) + 1)
            for g in range(K):
                for wh in range(WH):
                    o = map_ps[g // 2][0:K * UNIT_ROWS, (g % 2) * W + wh * P:(g % 2) * W + (wh + 1) * P]
                    last = nc.tensor.transpose(
                        o, probs[:, wh, g * K:(g + 1) * K, :].rearrange("p k h -> p (k h)"), ident)
            last.then_inc(flipped, 1)

        def unit(img, it, first_unit):
            for rr in range(UNIT_ROWS):
                scan_row(img, rr, first_unit, it)
                if first_unit and rr == TILE_ROWS and not first_image(img):
                    pe.wait_ge(collected, groups(img - 2, GROUP_COUNT))
                    pe.wait_ge(collected_act, act_groups(img - 2, STRIPS * (GROUPS - 1)))
                if not first_unit:
                    if rr == TILE_ROWS - 1:
                        shift(img, it - 1)
                    if rr == 3 * TILE_ROWS - 1:
                        flip(img, it - 1)

        def blending_done(img):
            pe.wait_ge(copied, pairs(img - 2, PAIR_COUNT))
            pe.wait_ge(banded, groups(img - 2, GROUP_COUNT))

        def scan(img):
            if not first_image(img):
                blending_done(img)
                pe.wait_ge(lifted, img * BLOCKS)
            unit(img, 0, True)
            with pe.Fori(1, UNITS) as it:
                unit(img, it, False)
            shift(img, UNITS - 1)
            flip(img, UNITS - 1)

        def cross(img, j, m, n, slot, signal=1):
            pe.wait_ge(copied, pairs(img, n - 1))
            for patch in range(2):
                for c in range(CH):
                    last = nc.tensor.transpose(
                        turn_ps[slot % 2][0:IPIX, patch * C + c * P:patch * C + (c + 1) * P],
                        patches[j][:, c, 2 * m + patch, :], ident)
            last.then_inc(crossed, signal)

        def spread(img, j, g, n):
            pe.wait_ge(banded, groups(img, n - 1))
            k = min(GROUP, PATCHES - g * GROUP)
            o = spread_ps[g % 2][0:IPIX, 0:k * PIX].rearrange("p (q y z) -> p q y z", q=k, y=PR)
            col = g * GROUP * PC
            src = kw[j][:, :, col:col + k * PC].rearrange("p y (q z) -> p q y z", q=k)
            for phase in range(K):
                last = nc.tensor.matmul(o[:, :, phase::K, :], spread_sb[:, phase, :], src[:, :, phase::K, :],
                                        start=True, stop=True, skip_group_check=True)
            last.then_inc(spreaded, 1)

        def multiply(img, m, n, slot, rows, signal):
            g = 2 * m // GROUP
            taken = (rows + 2) * IC
            pe.wait_ge(copied, pairs(img, n + 1))
            for patch in range(2):
                at = 2 * m + patch - g * GROUP
                cols = PC if 2 * m + patch < PATCHES - 1 else LAST_COLS
                for c in range(CH):
                    o = blend_ps[g % 2][c][:, at * PIX:(at + 1) * PIX].rearrange("p (y z) -> p y z", y=PR)
                    last = nc.tensor.matmul(
                        o[:, 0:rows, 0:cols], turned[slot % TURN][0:taken, patch, c * P:(c + 1) * P],
                        band[g % 2][0:taken, at, 0:rows, 0:cols], start=True, stop=True, skip_group_check=True)
            last.then_inc(blended, signal)

        def strip(img, t, slot, kw_uses, rows=PR):
            tail = rows < PR
            pair0, group0 = t * PAIRS, t * GROUPS
            for m in range(PAIRS):
                g = 2 * m // GROUP
                if 2 * m == g * GROUP:
                    if g + 1 < GROUPS:
                        spread(img, slot % 2, g + 1, group0 + g + 1)
                    elif not tail:
                        pe.wait_ge(kw_in[(slot + 1) % 2], 16 * kw_uses)
                        spread(img, (slot + 1) % 2, 0, group0 + GROUPS)
                    pe.wait_ge(banded, groups(img, group0 + g + 1))
                    pe.wait_ge(collected, groups(img, group0 + g - 1))
                    if g != 1:
                        pe.wait_ge(collected_act, act_groups(img, t * (GROUPS - 1) + max(g - 1, 0)))
                n = pair0 + m
                if m + 1 < PAIRS:
                    cross(img, slot % 2, m + 1, n + 1, slot * PAIRS + m + 1, 2 if tail and m + 2 == PAIRS else 1)
                elif not tail:
                    pe.wait_ge(windowed, strips(img, t + 2))
                    cross(img, (slot + 1) % 2, 0, n + 1, slot * PAIRS + m + 1)
                multiply(img, m, n, slot * PAIRS + m, rows, 2 if tail and m + 1 == PAIRS else 1)

        def blend(img, last):
            scans = img + 1 if last else img + 2
            pe.wait_ge(mapped, 2 * scans * UNITS + 1)
            pe.wait_ge(kw_in[0], 16 * (img * uses(2, 0) + 1))
            pe.wait_ge(spread_ready, 2)
            spread(img, 0, 0, 0)
            pe.wait_ge(windowed, strips(img, 1))
            cross(img, 0, 0, 0, 0)
            with pe.Fori(0, TURNS) as turn:
                for slot in range(TURN):
                    j = (slot + 1) % 2
                    strip(img, turn * TURN + slot, slot,
                          img * uses(2, j) + turn * (TURN // 2) + (slot + 1) // 2 + 1)
            strip(img, STRIPS - 1, 0, None, TAIL_ROWS)

        pe.wait_ge(const_in, 64)
        for c in range(CH):
            last = nc.tensor.matmul(banks[7][:, c * TAPS:(c + 1) * TAPS], comp_sb[:, c * P:(c + 1) * P],
                                    gen_sb[:], start=True, stop=True, skip_group_check=True)
        last.then_inc(taps_made, 1)
        pe.wait_ge(taps_copied, 1)
        schedule(pe, scan, blend)

    @block.scalar
    def _(act):
        def lift(img, u, par):
            act.wait_ge(shifted, img * UNITS + u + 1)
            for wh in range(WH):
                last = nc.scalar.copy(
                    rowsum[:, wh, par * BLOCK_ROWS:(par + 1) * BLOCK_ROWS, :],
                    gather_ps[par][wh][:, 0:BLOCK_ROWS * JK].rearrange("p (y t) -> p y t", t=JK))
            last.then_inc(lifted, 1)

        def exponent(img, u):
            act.wait_ge(centered, img * UNITS + u + 1)
            nc.scalar.activation(logits[:], logits[:], ACT.Exp).then_inc(powered, 1)

        def map_out(img, u):
            n = img * UNITS + u
            act.wait_ge(flipped, n + 2)
            act.wait_ge(planes_stored, 48 * n + 16)
            nc.scalar.copy(map_rows[:, 0:2, :], map_ps[0][0:K * UNIT_ROWS, :].rearrange(
                "p (g w) -> p g w", g=2)).then_inc(mapped, 1)
            nc.scalar.copy(map_rows[:, 2, :], map_ps[1][0:K * UNIT_ROWS, 0:W]).then_inc(mapped, 1)
            act.wait_ge(mapped, 2 * n + 3)
            dst = planes[bass.ds(img, 1)].rearrange("n k h w -> (n k) h w")
            for g in range(K):
                act.dma_start(dst[g * K:(g + 1) * K, bass.ds(u * UNIT_ROWS, UNIT_ROWS), :],
                              map_rows[:, g, :]).then_inc(planes_stored, 16)

        def scan(img):
            act.wait_ge(gathered, img * (BLOCKS - 1) + 1)
            lift(img, 0, 0)
            with act.Fori(1, UNITS) as it:
                act.wait_ge(gathered, img * (BLOCKS - 1) + 2 * it)
                lift(img, it - 1, 1)
                exponent(img, it - 1)
                act.wait_ge(gathered, img * (BLOCKS - 1) + 2 * it + 1)
                lift(img, it, 0)
                map_out(img, it - 1)
            act.wait_ge(scanned, (img + 1) * TILES)
            lift(img, UNITS - 1, 1)
            exponent(img, UNITS - 1)
            map_out(img, UNITS - 1)

        def collect(img, t, slot, g, stores, rows):
            act.wait_ge(blended, pairs(img, t * PAIRS + group_end(g)))
            if g == 0:
                act.wait_ge(stored[slot % 2], 16 * (stores + 1))
            nc.scalar.copy(
                out_rows[slot % 2][:, 1, 0:rows, g * GROUP * PC:(g + 1) * GROUP * PC].rearrange(
                    "p y (q z) -> p q y z", q=GROUP),
                blend_ps[g % 2][1][:, 0:GROUP * PIX].rearrange(
                    "p (q y z) -> p q y z", q=GROUP, y=PR)[:, :, 0:rows]).then_inc(collected_act, 1)

        def strip(img, t, slot, stores, rows=PR):
            tail = rows < PR
            for m in range(PAIRS):
                n, at = t * PAIRS + m, slot * PAIRS + m
                act.wait_ge(crossed, pairs(img, n + 1))
                act.wait_ge(blended, pairs(img, n + 1 - TURN))
                nc.scalar.copy(turned[at % TURN][0:IPIX].rearrange("p a c -> p (a c)"),
                               turn_ps[at % 2][0:IPIX, :]).then_inc(copied, 2 if tail and m + 1 == PAIRS else 1)
                for g in range(GROUPS - 1):
                    if m == group_end(g) + 1:
                        collect(img, t, slot, g, stores, rows)

        def blend(img, last):
            with act.Fori(0, TURNS) as turn:
                for slot in range(TURN):
                    strip(img, turn * TURN + slot, slot,
                          img * uses(2, slot % 2) + turn * (TURN // 2) + slot // 2)
            strip(img, STRIPS - 1, 0, img * uses(2, 0) + STRIPS // 2, TAIL_ROWS)

        schedule(act, scan, blend)

    @block.vector
    def _(dve):
        def softmax(img, u):
            n = img * UNITS + u
            dve.wait_ge(shifted, n + 2)
            bias = bias_sb[:].unsqueeze(1).to_broadcast((P, UNIT_ROWS, KK))
            for wh in range(WH):
                nc.vector.tensor_tensor(
                    logits[:, wh * UNIT_ROWS:(wh + 1) * UNIT_ROWS, :],
                    logit_ps[wh][:, 0:UNIT_ROWS * KK].rearrange("p (y k) -> p y k", k=KK),
                    bias, ALU.add).then_inc(logits_taken, 1)
            dve.wait_ge(logits_taken, 2 * n + 3)
            nc.vector.reduce_max(top[:], logits[:], AX.X).then_inc(topped, 1)
            dve.wait_ge(topped, n + 1)

            def per_pixel(a):
                return a[:].unsqueeze(2).to_broadcast((P, WH * UNIT_ROWS, KK))
            nc.vector.tensor_tensor(logits[:], logits[:], per_pixel(top), ALU.subtract).then_inc(centered, 1)
            dve.wait_ge(powered, n + 1)
            nc.vector.reduce_sum(total[:], logits[:], AX.X).then_inc(totalled, 1)
            dve.wait_ge(totalled, n + 1)
            nc.vector.reciprocal(scale[:], total[:]).then_inc(inverted, 1)
            dve.wait_ge(inverted, n + 1)
            dve.wait_ge(flipped, n + 1)
            for wh in range(WH):
                rows = slice(wh * UNIT_ROWS, (wh + 1) * UNIT_ROWS)
                last = nc.vector.tensor_tensor(
                    probs[:, wh].rearrange("p k y -> p y k"), logits[:, rows, :],
                    scale[:, rows].unsqueeze(2).to_broadcast((P, UNIT_ROWS, KK)), ALU.mult)
            last.then_inc(probs_made, 1)

        def scan(img):
            with dve.Fori(0, UNITS) as u:
                softmax(img, u)

        def matrix(img, g, n, pair_end):
            k = min(GROUP, PATCHES - g * GROUP)
            dve.wait_ge(spreaded, groups(img, n + 1))
            dve.wait_ge(blended, pairs(img, pair_end))
            nc.vector.tensor_tensor(
                band[g % 2][0:IPIX, 0:k].rearrange("p q y z -> p q (y z)"),
                spread_ps[g % 2][0:IPIX, 0:k * PIX].rearrange("p (q o) -> p q o", q=k),
                mask[0:IPIX].rearrange("p y z -> p (y z)").unsqueeze(1).to_broadcast((IPIX, k, PIX)),
                ALU.mult).then_inc(banded, 1)

        def collect(img, t, slot, g, stores, rows):
            tail = rows < PR
            end = group_end(g) + (1 if tail and g == GROUPS - 1 else 0)
            dve.wait_ge(blended, pairs(img, t * PAIRS + end))
            if g == 0:
                dve.wait_ge(stored[slot % 2], 16 * (stores + 1))
            first = g * GROUP
            full = min(GROUP, PATCHES - 1 - first)
            for c in range(1 if g < GROUPS - 1 else CH):
                ps = blend_ps[g % 2][c]
                last = nc.vector.tensor_copy(
                    out_rows[slot % 2][:, c, 0:rows, first * PC:(first + full) * PC].rearrange(
                        "p y (q z) -> p q y z", q=full),
                    ps[:, 0:full * PIX].rearrange("p (q y z) -> p q y z", q=full, y=PR)[:, :, 0:rows])
                if full < GROUP:
                    at = full * PIX
                    last = nc.vector.tensor_copy(
                        out_rows[slot % 2][:, c, 0:rows, (first + full) * PC:W],
                        ps[:, at:at + PIX].rearrange("p (y z) -> p y z", y=PR)[:, 0:rows, 0:LAST_COLS])
            last.then_inc(collected, 1)

        def lay_inner(q, j, c, row, to, rows):
            src = xs[q][:, c, row:row + rows, PC - 1:]
            src = bass.AP(src.tensor, src.offset, [src.ap[0], [PC, PATCHES - 2], [W, rows], [1, IC]])
            return nc.vector.tensor_copy(
                patches[j][:, c, 1:PATCHES - 1, to * IC:(to + rows) * IC].rearrange(
                    "p q (r s) -> p q r s", r=rows), src)

        def lay_outer(q, j, row, to, rows):
            src = xs[q][:, :, row:row + rows]
            dst = patches[j][:, :, :, to * IC:(to + rows) * IC].rearrange("p c q (r s) -> p c q r s", r=rows)
            right = (PATCHES - 1) * PC - 1
            nc.vector.tensor_copy(dst[:, :, 0, :, 1:IC], src[:, :, :, 0:IC - 1])
            nc.vector.tensor_copy(dst[:, :, PATCHES - 1, :, 0:W - right], src[:, :, :, right:W])
            for col, at, patch in ((1, 0, 0), (W - 2, W - right, PATCHES - 1)):
                last = nc.vector.tensor_copy(dst[:, :, patch, :, at], src[:, :, :, col])
            return last

        def lay_part(img, t, slot, part):
            q, j = slot % SLOTS, slot % 2
            if part == 0:
                dve.wait_ge(crossed, pairs(img, (t - 1) * PAIRS))
                dve.wait_ge(windowed, strips(img, t))
                nc.vector.tensor_copy(patches[j][:, :, :, 0:2 * IC], patches[1 - j][:, :, :, PR * IC:IR * IC])
            if part == 1:
                lay_inner(q, j, 0, 1, 2, PR)
            if part == 2:
                lay_inner(q, j, 1, 1, 2, PR)
                lay_outer(q, j, 1, 2, PR).then_inc(windowed, 1)

        def lay_first(img):
            dve.wait_ge(strip_in[0], 32 * (img * uses(SLOTS, 0) + 1))
            dve.wait_ge(crossed, pairs(img, 0))
            for row, to, rows in ((1, 0, 1), (0, 1, 1), (1, 2, PR)):
                for c in range(CH):
                    lay_inner(0, 0, c, row, to, rows)
                last = lay_outer(0, 0, row, to, rows)
            last.then_inc(windowed, 1)

        def strip(img, t, slot, stores, loads, rows=PR):
            tail = rows < PR
            for g in range(GROUPS):
                before = t * PAIRS + (group_end(g - 1) if g else 0)
                if g + 1 < GROUPS:
                    matrix(img, g + 1, t * GROUPS + g + 1, before)
                elif not tail:
                    matrix(img, 0, (t + 1) * GROUPS, before)
                collect(img, t, slot, g, stores, rows)
                if not tail and g < GROUPS - 1:
                    if g == 0:
                        dve.wait_ge(strip_in[(slot + 1) % SLOTS], loads)
                    lay_part(img, t + 1, slot + 1, g)

        def blend(img, last):
            lay_first(img)
            matrix(img, 0, 0, 0)
            with dve.Fori(0, TURNS) as turn:
                for slot in range(TURN):
                    nxt = (slot + 1) % SLOTS
                    strip(img, turn * TURN + slot, slot,
                          img * uses(2, slot % 2) + turn * (TURN // 2) + slot // 2,
                          32 * (img * uses(SLOTS, nxt) + turn + (slot + 1) // SLOTS + 1))
            strip(img, STRIPS - 1, 0, img * uses(2, 0) + STRIPS // 2, None, TAIL_ROWS)
            dve.wait_ge(windowed, strips(img, STRIPS))
            nc.vector.memset(primer[:, 31:32], 0.0).then_inc(windowed, 1)

        for j in range(2):
            last = nc.vector.memset(patches[j][:, :, PATCHES - 1, :], 0.0)
        last.then_inc(spread_ready, 1)
        dve.wait_ge(const_in, 64)
        nc.vector.tensor_copy(spread_sb[:].rearrange("p a b -> p (a b)"), spread32).then_inc(spread_ready, 1)
        dve.wait_ge(taps_made, 1)
        nc.vector.tensor_copy(taps_sb[:].rearrange("p c t -> p (c t)"),
                              banks[7][:, 0:CH * TAPS]).then_inc(taps_copied, 1)
        for at, (signal, n) in enumerate((
                (shifted, 1), (logits_taken, 1), (flipped, 1), (mapped, 1), (planes_stored, 16),
                (stored[0], 16), (stored[1], 16), (crossed, PAIR_COUNT), (copied, PAIR_COUNT),
                (blended, PAIR_COUNT), (spreaded, GROUP_COUNT), (banded, GROUP_COUNT),
                (collected, GROUP_COUNT), (collected_act, STRIPS * (GROUPS - 1)), (windowed, STRIP_COUNT))):
            nc.vector.memset(primer[:, at:at + 1], 0.0).then_inc(signal, n)
        schedule(dve, scan, blend)

    @block.gpsimd
    def _(pool):
        STEPS_A_CHUNK = 17

        def number(name, n=CHUNK):
            at = NUMBERS.index(name)
            return numbers[:, at:at + 1].to_broadcast((P, n))


        def chunk(img, ht, wc):
            n = img * CHUNKS + ht * (W // CHUNK) + wc
            count = n * STEPS_A_CHUNK
            done = 0

            def step(instruction):
                nonlocal done
                done += 1
                instruction.then_inc(refining, 1)
                pool.wait_ge(refining, count + done)

            w0 = wc * CHUNK
            nc.gpsimd.dma_start(raw[:].rearrange("p w k -> p (w k)"),
                                reread[bass.ds(img, 1)].rearrange("n h q -> (n h) q")[
                                    ht * P:(ht + 1) * P, w0 * KK:(w0 + CHUNK) * KK]).then_inc(raw_in, 16)
            pool.wait_ge(raw_in, 16 * (n + 1))
            for phase in range(K):
                first = (phase - w0) % K
                cols = slice(first, CHUNK, K)
                count_w = len(range(first, CHUNK, K))
                for j in range(K):
                    plane = (j + phase) % K
                    last = nc.gpsimd.tensor_tensor(
                        weighed[:, plane::K, cols],
                        raw[:, cols, j::K].rearrange("p w i -> p i w"),
                        window[:, :, j:j + 1].to_broadcast((P, K, count_w)), ALU.mult)
            step(last)
            sum4 = coef[:, 0:4]
            step(nc.gpsimd.tensor_tensor(sum4, weighed[:, 0:4], weighed[:, 4:8], ALU.add))
            sum2 = coef[:, 4:6]
            step(nc.gpsimd.tensor_tensor(sum2, sum4[:, 0:2], sum4[:, 2:4], ALU.add))
            step(nc.gpsimd.tensor_tensor(norm[:, 0], sum2[:, 0], sum2[:, 1], ALU.add))
            step(nc.gpsimd.tensor_tensor(norm[:, 1], norm[:, 0], weighed[:, 8], ALU.add))
            step(nc.gpsimd.tensor_tensor(norm[:, 0], norm[:, 1], number("eps"), ALU.add))
            step(nc.gpsimd.tensor_tensor(norm[:, 1], norm[:, 0], number("-1"), ALU.pow))
            step(nc.gpsimd.tensor_tensor(norm[:, 2], norm[:, 0], norm[:, 1], ALU.mult))
            step(nc.gpsimd.tensor_tensor(norm[:, 3], norm[:, 2], number("-2"), ALU.add))
            step(nc.gpsimd.tensor_tensor(norm[:, 0], norm[:, 1], norm[:, 3], ALU.mult))
            step(nc.gpsimd.tensor_tensor(coef[:], weighed[:], norm[:, 0:1].to_broadcast((P, KK, CHUNK)), ALU.mult))
            for phase in range(K):
                first = (phase - w0) % K
                centre = K + (1 + phase) % K
                mine = coef[:, centre, first::K]
                last = nc.gpsimd.tensor_tensor(mine, mine, number("2", mine.shape[1]), ALU.add)
            step(last)
            if ht or wc:
                pool.wait_ge(coefs_stored, 16 * n)
            high, mid, low = (pieces[:, part * KK:(part + 1) * KK] for part in range(PARTS))
            nothing = number("0").unsqueeze(1).to_broadcast((P, KK, CHUNK))
            step(nc.gpsimd.tensor_tensor(high, coef[:], nothing, ALU.add))
            step(nc.gpsimd.tensor_tensor(weighed[:], coef[:], high, ALU.subtract))
            step(nc.gpsimd.tensor_tensor(mid, weighed[:], nothing, ALU.add))
            step(nc.gpsimd.tensor_tensor(coef[:], weighed[:], mid, ALU.subtract))
            step(nc.gpsimd.tensor_tensor(low, coef[:], nothing, ALU.add))
            assert done == STEPS_A_CHUNK, done
            nc.gpsimd.dma_start(
                coefs[bass.ds(img, 1)].rearrange("n q h w -> h (n q) w")[ht * P:(ht + 1) * P, :, w0:w0 + CHUNK],
                pieces[:]).then_inc(coefs_stored, 16)

        for j in range(2):
            last = nc.gpsimd.memset(kw[j][:], 0.0)
        last.then_inc(cleared, 1)
        pool.wait_ge(const_in, 64)
        with pool.Fori(0, images) as img:
            for ht in range(H // P):
                for wc in range(W // CHUNK):
                    if ht == 0 and wc == 0:
                        pool.wait_ge(planes_stored, 48 * UNITS * (img + 1) + 16)
                    chunk(img, ht, wc)
            pool.wait_ge(coefs_stored, 16 * CHUNKS * (img + 1))


_INS = ["x", "w_comp", "w_gen", "b_gen", "const"]


def program(nc, shapes):
    from contextlib import ExitStack
    f32 = mybir.dt.float32
    args = {n: nc.dram_tensor(n, shapes[n], f32, kind="ExternalInput").ap() for n in _INS}
    out = nc.dram_tensor("out", shapes["x"], f32, kind="ExternalOutput").ap()
    with ExitStack() as ctx:
        build(nc, ctx, *(args[n] for n in _INS), out, images=shapes["x"][0])


def kernel(x, L0_conv_w_comp, L0_conv_w_gen, L0_conv_b_gen):
    import concourse.bacc as bacc
    from concourse.bass_utils import run_bass_kernel_spmd

    gen = np.asarray(L0_conv_w_gen).transpose(1, 2, 3, 0)[:, ::-1].reshape(COMP, TAPS)
    arrays = {
        "x": np.ascontiguousarray(x),
        "w_comp": np.ascontiguousarray(L0_conv_w_comp),
        "w_gen": np.ascontiguousarray(gen),
        "b_gen": np.ascontiguousarray(L0_conv_b_gen).reshape(1, KK),
        "const": constants(),
    }
    nc = bacc.Bacc("TRN2", target_bir_lowering=False, num_devices=1)
    program(nc, {n: a.shape for n, a in arrays.items()})
    result = run_bass_kernel_spmd(nc, [arrays], core_ids=[0])
    return result.results[0]["out"]
```

```python
import numpy as np

import concourse.bass as bass
import concourse.mybir as mybir
from concourse.alu_op_type import AluOpType as ALU

B, C, H, W = 4, 256, 256, 256
COMP = 64
K = 3
KK = K * K
P = 128
CH = C // P
WH = W // P

TILE_ROWS = 8
SLOTS = 4
UNIT_ROWS = TILE_ROWS * SLOTS
UNITS = H // UNIT_ROWS
TILES = H // TILE_ROWS
BLOCK_ROWS = 16
BLOCKS = H // BLOCK_ROWS
SLOTS_OF_SUMS = BLOCK_ROWS + 2
JK = K * KK
TAPS = K * JK
TAP_COLS = 512 - (BLOCK_ROWS - 1) * JK & ~1

CHUNK = 128
CHUNKS = (H // P) * (W // CHUNK)

SR, PC = 16, 12
TR = 9
IC = PC + 2
IPIX = TR * IC
TILED = 2
REACH = [0, SR - TR]
IR = TILED * TR
STRIPS = H // SR
PATCHES = -(-W // PC)
PAIRS = PATCHES // 2
PAIR_COLS = 2 * PC
LAST_COLS = W - (PAIRS - 1) * PAIR_COLS
KW_PITCH = PATCHES * PC
PARTS = 3

UNIT_COUNT = STRIPS * CH
PAIR_COUNT = UNIT_COUNT * PAIRS
BAND_COUNT = STRIPS * PAIRS
assert STRIPS * SR == H and IR == SR + 2 and IPIX <= P and CH == 2 and PAIRS % 2 == 1
assert TILED * TR * PAIR_COLS <= 512 and SLOTS_OF_SUMS * JK <= 512


NUMBERS = ["eps", "-2", "-1", "0", "2"]


def constants():
    ident = np.eye(P)
    from_left = np.eye(P, k=1)
    from_right = np.eye(P, k=-1)
    carry_left = np.zeros((P, P))
    carry_left[P - 1, 0] = 1
    carry_right = np.zeros((P, P))
    carry_right[0, P - 1] = 1
    spread = np.zeros((P, K, P))
    mask = np.zeros((P, TILED, TR, 2, PC))
    for r in range(TR):
        for s in range(IC):
            for phase in range(K):
                for part in range(PARTS):
                    spread[part * KK + (r - phase) % K * K + s % K, phase, r * IC + s] = 1
            for tile in range(TILED):
                for y in range(TR):
                    for z in range(PC):
                        i = tile * TR + r - REACH[tile] - y
                        mask[r * IC + s, tile, y, :, z] = 0 <= i < K and 0 <= s - z < K
    window = np.broadcast_to(np.outer(np.hamming(K), np.hamming(K)).reshape(-1), (P, KK))
    values = np.broadcast_to([1e-8 if n == "eps" else float(n) for n in NUMBERS], (P, len(NUMBERS)))
    return np.concatenate([ident, from_left, from_right, carry_left, carry_right,
                           spread.reshape(P, -1), mask.reshape(P, -1), window, values],
                          1).astype(np.float32)


def build(nc, ctx, x, w_comp, w_gen, b_gen, const, out, images=B):
    f32, bf16 = mybir.dt.float32, mybir.dt.bfloat16
    ACT = mybir.ActivationFunctionType
    AX = mybir.AxisListType

    def sb(name, shape, dt=f32):
        return ctx.enter_context(nc.sbuf_tensor(name, shape, dt))

    def sem(name):
        return ctx.enter_context(nc.semaphore(name))

    planes = nc.dram_tensor("planes", (images, KK, H, W), f32).ap()
    coefs = nc.dram_tensor("coefs", (images, PARTS * KK, H, W), bf16).ap()
    reread = planes.rearrange("n k h w -> n (k h w)").rearrange("n (h q) -> n h q", q=W * KK)

    x_rows = [sb(f"x_rows{c}", [P, CH * TILE_ROWS * W]) for c in range(CH)]
    patch_rows = [sb(f"patch_rows{c}", [P, PATCHES * IR * IC]) for c in range(CH)]
    tiles = [t[:, 0:CH * TILE_ROWS * W].rearrange("p (c h w) -> p c h w", c=CH, h=TILE_ROWS)
             for t in (*x_rows, *patch_rows)]
    halves = [t[:].rearrange("p (h w) -> p h w", h=SR) for t in x_rows]
    patches = [t[:].rearrange("p (q o) -> p q o", q=PATCHES) for t in patch_rows]
    first_row = sb("first_row", [P, CH, W])
    kw = sb("kw_strip", [P, SR, KW_PITCH], bf16)
    out_rows = [sb(f"out_rows{c}", [P, SR, W]) for c in range(CH)]
    const_sb = sb("const_sb", [P, const.shape[1]])
    spread_sb = sb("spread_sb", [P, K, P], bf16)
    comp_sb = sb("comp_sb", [COMP, C])
    gen_sb = sb("gen_sb", [COMP, TAPS])
    bias_sb = sb("bias_sb", [P, KK])
    taps_sb = sb("taps_sb", [P, CH, TAP_COLS])
    rowsum = sb("rowsum", [P, WH, UNIT_ROWS, JK])
    carry = [sb(f"carry{par}", [P, WH, JK]) for par in range(2)]
    logits = sb("logits", [P, WH * UNIT_ROWS, KK])
    top = sb("top", [P, WH * UNIT_ROWS])
    total = sb("total", [P, WH * UNIT_ROWS])
    scale = sb("scale", [P, WH * UNIT_ROWS])
    probs = sb("probs", [P, WH, KK, UNIT_ROWS])
    map_rows = sb("map_rows", [K * UNIT_ROWS, K, W])
    turned = [sb(f"turned{j}", [P, 2, TILED, P]) for j in range(2)]
    band = sb("band", [P, PAIRS, TILED, TR, PAIR_COLS])
    raw = sb("raw", [P, CHUNK, KK])
    weighed = sb("weighed", [P, KK, CHUNK])
    coef = sb("coef", [P, KK, CHUNK])
    pieces = sb("pieces", [P, PARTS * KK, CHUNK], bf16)
    norm = sb("norm", [P, 4, CHUNK])
    primer = sb("primer", [P, 32])

    at = 0
    def const_part(n):
        nonlocal at
        at += n
        return const_sb[:, at - n:at]
    ident, from_left, from_right, carry_left, carry_right = (const_part(P) for _ in range(5))
    spread32 = const_part(K * P)
    mask = const_part(TILED * TR * PAIR_COLS)
    window = const_part(KK).rearrange("p (i j) -> p i j", i=K)
    numbers = const_part(len(NUMBERS))

    banks = [ctx.enter_context(nc.psum_tensor(f"bank{n}", [P, 512], f32)) for n in range(8)]
    gather_ps = [[banks[2 * par + wh] for wh in range(WH)] for par in range(2)]
    logit_ps = banks[4:6]
    map_ps = banks[6:8]
    turn_ps = banks[0:2]
    spread_ps = banks[2:4]
    blend_ps = banks[4:6]

    const_in = sem("const_in")
    cleared = sem("cleared")
    spread_ready = sem("spread_ready")
    taps_made = sem("taps_made")
    taps_copied = sem("taps_copied")
    tile_in = [sem(f"tile_in{q}") for q in range(SLOTS)]
    scanned = sem("scanned")
    summed = sem("summed")
    lifted = sem("lifted")
    shifted = sem("shifted")
    logits_taken = sem("logits_taken")
    biased = sem("biased")
    topped = sem("topped")
    centered = sem("centered")
    powered = sem("powered")
    totalled = sem("totalled")
    inverted = sem("inverted")
    probs_made = sem("probs_made")
    flipped = sem("flipped")
    mapped = sem("mapped")
    planes_stored = sem("planes_stored")
    raw_in = sem("raw_in")
    refining = sem("refining")
    coefs_stored = sem("coefs_stored")
    first_in = sem("first_in")
    x_in = [sem(f"x_in{c}") for c in range(CH)]
    kw_in = sem("kw_in")
    haloed = sem("haloed")
    laid = sem("laid")
    crossed = sem("crossed")
    copied = sem("copied")
    spreaded = sem("spreaded")
    banded = sem("banded")
    blended = sem("blended")
    collected = sem("collected")
    collected_act = sem("collected_act")
    collected_last = sem("collected_last")
    stored = [sem(f"stored{c}") for c in range(CH)]

    def first_image(img):
        return isinstance(img, int) and img == 0

    def units(img, s, c=0):
        return (img + 1) * UNIT_COUNT + s * CH + c

    def pairs(img, s, c=0, m=0):
        return (img + 1) * PAIR_COUNT + s * (CH * PAIRS) + (c * PAIRS + m)

    def bands(img, s, m=0):
        return (img + 1) * BAND_COUNT + s * PAIRS + m

    def act_pairs(img, s, m=0):
        return (img + 1) * STRIPS * (PAIRS - 1) + s * (PAIRS - 1) + m

    def strips(img, s):
        return (img + 1) * STRIPS + s

    def ahead(eng, register, value):
        if isinstance(value, int):
            return value
        eng.reg_mov(register, value)
        return register

    block = ctx.enter_context(nc.Block())

    def schedule(eng, scan, blend):
        scan(0)
        if images > 1:
            with eng.Fori(0, images - 1) as n:
                scan(n + 1)
                blend(n, False)
        blend(images - 1, True)

    @block.sync
    def _(sp):
        second_wait = sp.alloc_register("second_wait")

        def load_tile(img, it, q):
            src = x[bass.ds(img, 1)].rearrange("n (c p) h w -> p c (n h) w", c=CH)
            for c in range(CH):
                nc.sync.dma_start(tiles[q][:, c], src[:, c, bass.ds((it * SLOTS + q) * TILE_ROWS, TILE_ROWS), :])\
                    .then_inc(tile_in[q], 16)

        def scan(img):
            for q in range(SLOTS):
                if not first_image(img):
                    if q < CH:
                        blend_through = ahead(sp, second_wait, units(img - 2, STRIPS - 1, q + 1))
                    else:
                        blend_through = ahead(sp, second_wait, pairs(img - 2, STRIPS - 1, q + 1 - CH))
                    sp.wait_ge(scanned, img * TILES)
                    sp.wait_ge(laid if q < CH else crossed, blend_through)
                load_tile(img, 0, q)
            with sp.Fori(1, UNITS) as it:
                for q in range(SLOTS):
                    sp.wait_ge(scanned, img * TILES + (it - 1) * SLOTS + q + 1)
                    load_tile(img, it, q)

        def load_half(img, s, c):
            src = x[bass.ds(img, 1)].rearrange("n (c p) h w -> p c (n h) w", c=CH)[:, c]
            rows = SR // 2
            for n in range(2):
                nc.sync.dma_start(halves[c][:, n * rows:(n + 1) * rows],
                                  src[:, bass.ds(s * SR + 1 + n * rows, rows), :]).then_inc(x_in[c], 16)

        def load_last_half(img, c):
            src = x[bass.ds(img, 1)].rearrange("n (c p) h w -> p c (n h) w", c=CH)[:, c]
            nc.sync.dma_start(halves[c][:, 0:SR - 1], src[:, H - SR + 1:H, :]).then_inc(x_in[c], 16)
            nc.sync.dma_start(halves[c][:, SR - 1], src[:, H - 2, :]).then_inc(x_in[c], 16)

        def load_kw(img, s):
            src = coefs[bass.ds(img, 1)].rearrange("n p h w -> p (n h) w")
            nc.sync.dma_start(kw[0:PARTS * KK, :, 0:W], src[:, bass.ds(s * SR, SR), :]).then_inc(kw_in, 16)

        def store(img, s, c):
            at = img * (C * H * W) + (s * (SR * W) + c * (P * H * W))
            dst = bass.AP(out.tensor, at, [[H * W, P], [1, SR * W]])
            if c == 0:
                sp.wait_ge(collected, bands(img, s + 1))
            else:
                last_done = ahead(sp, second_wait, strips(img, s + 1))
                sp.wait_ge(collected_act, act_pairs(img, s + 1))
                sp.wait_ge(collected_last, last_done)
            nc.sync.dma_start(dst, out_rows[c][:].rearrange("p y w -> p (y w)")).then_inc(stored[c], 16)

        def strip(img, s, load, kw_load):
            for c in range(CH):
                if load:
                    sp.wait_ge(laid, units(img, s, c + 1))
                    load(c)
            store(img, s, 0)
            if kw_load:
                sp.wait_ge(spreaded, bands(img, s + 2))
                load_kw(img, s + 2)
            store(img, s, 1)

        def blend(img, last):
            if last and images > 1:
                sp.wait_ge(laid, units(img, 0))
            else:
                sp.wait_ge(scanned, (img + 1 if last else img + 2) * TILES)
            src = x[bass.ds(img, 1)].rearrange("n (c p) h w -> p c (n h) w", c=CH)
            nc.sync.dma_start(first_row[:], src[:, :, 0, :]).then_inc(first_in, 16)
            for c in range(CH):
                load_half(img, 0, c)
            sp.wait_ge(coefs_stored, 16 * CHUNKS * (img + 1))
            sp.wait_ge(cleared, 1)
            load_kw(img, 0)
            sp.wait_ge(spreaded, bands(img, 1))
            load_kw(img, 1)
            with sp.Fori(0, STRIPS - 2) as s:
                strip(img, s, lambda c: load_half(img, s + 1, c), True)
            strip(img, STRIPS - 2, lambda c: load_last_half(img, c), False)
            strip(img, STRIPS - 1, None, False)

        nc.sync.dma_start(const_sb[:], const).then_inc(const_in, 16)
        nc.sync.dma_start(comp_sb[:], w_comp).then_inc(const_in, 16)
        nc.sync.dma_start(gen_sb[:], w_gen).then_inc(const_in, 16)
        nc.sync.dma_start(bias_sb[:], b_gen[0:1, :].to_broadcast((P, KK))).then_inc(const_in, 16)
        schedule(sp, scan, blend)
        for slot in range(2):
            sp.wait_ge(stored[slot], 16 * (1 + images * STRIPS))

    @block.tensor
    def _(pe):
        def scan_row(img, rr, it):
            q, row = divmod(rr, TILE_ROWS)
            par, yy = divmod(rr, BLOCK_ROWS)
            if row == 0:
                pe.wait_ge(tile_in[q], 32 * (img * UNITS + it + 1))
            if yy == 0 and not isinstance(it, int):
                pe.wait_ge(lifted, img * BLOCKS + 2 * it + par - 1)
            for wh in range(WH):
                for c in range(CH):
                    last = nc.tensor.matmul(
                        gather_ps[par][wh][:, yy * JK:yy * JK + TAP_COLS],
                        tiles[q][:, c, row, wh * P:(wh + 1) * P], taps_sb[:, c, :],
                        start=yy == 0 and c == 0, stop=yy == BLOCK_ROWS - 1 and c == CH - 1, skip_group_check=True)
            if row == TILE_ROWS - 1:
                last.then_inc(scanned, 1)

        def shift(img, u):
            if isinstance(u, int):
                pe.wait_ge(lifted, (img + 1) * BLOCKS)
            else:
                pe.wait_ge(summed, img * (UNITS - 1) + u + 1)
            pe.wait_ge(logits_taken, 2 * (img * UNITS + u) + 1)
            for wh in range(WH):
                o = logit_ps[wh][:, 0:UNIT_ROWS * KK]

                def tap(j, half):
                    return rowsum[:, half, :, j * KK:(j + 1) * KK]
                nc.tensor.matmul(o, from_left, tap(0, wh), start=True, stop=False)
                nc.tensor.matmul(o, from_right, tap(2, wh), start=False, stop=False)
                if wh == 0:
                    last = nc.tensor.matmul(o, carry_right, tap(2, 1), start=False, stop=True)
                else:
                    last = nc.tensor.matmul(o, carry_left, tap(0, 0), start=False, stop=True)
            last.then_inc(shifted, 1)

        def flip(img, u):
            pe.wait_ge(probs_made, img * UNITS + u + 1)
            pe.wait_ge(mapped, 2 * (img * UNITS + u) + 1)
            for g in range(K):
                for wh in range(WH):
                    o = map_ps[g // 2][0:K * UNIT_ROWS, (g % 2) * W + wh * P:(g % 2) * W + (wh + 1) * P]
                    last = nc.tensor.transpose(
                        o, probs[:, wh, g * K:(g + 1) * K, :].rearrange("p k h -> p (k h)"), ident)
            last.then_inc(flipped, 1)

        def unit(img, it):
            for rr in range(UNIT_ROWS):
                scan_row(img, rr, it)
                if isinstance(it, int):
                    if rr == TILE_ROWS and not first_image(img):
                        pe.wait_ge(collected, bands(img - 2, STRIPS))
                        pe.wait_ge(collected_last, strips(img - 2, STRIPS))
                else:
                    if rr == BLOCK_ROWS + 3:
                        shift(img, it - 1)
                    if rr == UNIT_ROWS - 1:
                        flip(img, it - 1)

        def scan(img):
            if not first_image(img):
                pe.wait_ge(copied, pairs(img - 2, STRIPS))
                pe.wait_ge(banded, bands(img - 2, STRIPS))
                pe.wait_ge(lifted, img * BLOCKS)
            unit(img, 0)
            with pe.Fori(1, UNITS) as it:
                unit(img, it)
            shift(img, UNITS - 1)
            flip(img, UNITS - 1)

        def cross(img, s, c, m):
            pe.wait_ge(copied, pairs(img, s, c, m - 1))
            if m == 0:
                pe.wait_ge(laid, units(img, s, c + 1))
            for patch in range(2):
                for tile in range(TILED):
                    at = (patch * TILED + tile) * P
                    last = nc.tensor.transpose(
                        turn_ps[(c * PAIRS + m) % 2][0:IPIX, at:at + P],
                        patches[c][:, 2 * m + patch, tile * IPIX:(tile + 1) * IPIX], ident)
            last.then_inc(crossed, 1)

        def spread(img, s, m):
            pe.wait_ge(banded, bands(img, s, m - 1 if m else 0))
            o = spread_ps[m % 2][:, 0:TILED * TR * PAIR_COLS].rearrange(
                "p (t y z) -> p t y z", t=TILED, y=TR)
            for phase in range(K):
                first = [next(y for y in range(r, SR) if y % K == phase) for r in REACH]
                stride = (first[1] - REACH[1] - first[0]) + TR
                src = bass.AP(kw, first[0] * KW_PITCH + m * PAIR_COLS,
                              [[SR * KW_PITCH, P], [(first[1] - first[0]) * KW_PITCH, TILED],
                               [K * KW_PITCH, TR // K], [1, PAIR_COLS]])
                dst = o[:, :, first[0]::K, :]
                dst = bass.AP(dst.tensor, dst.offset, [dst.ap[0], [stride * PAIR_COLS, TILED],
                                                       [K * PAIR_COLS, TR // K], [1, PAIR_COLS]])
                last = nc.tensor.matmul(dst, spread_sb[:, phase, :], src,
                                        start=True, stop=True, skip_group_check=True)
            last.then_inc(spreaded, 1)

        def multiply(img, s, c, m):
            pe.wait_ge(copied, pairs(img, s, c, m + 1))
            if c == 0:
                pe.wait_ge(banded, bands(img, s, m + 1))
            if m >= 2:
                if c == 0:
                    pe.wait_ge(collected, bands(img, s, m - 1))
                else:
                    pe.wait_ge(collected_act, act_pairs(img, s, m - 1))
            elif c == 1:
                pe.wait_ge(collected, bands(img, s, PAIRS - 1 + m))
            elif m == 0:
                pe.wait_ge(collected_act, act_pairs(img, s))
            else:
                pe.wait_ge(collected_last, strips(img, s))
            n = c * PAIRS + m
            o = blend_ps[n % 2][:, 0:SR * PAIR_COLS].rearrange("p (y q z) -> p y q z", y=SR, q=2)
            for patch in range(2):
                for tile in range(TILED):
                    rows = slice(REACH[tile], REACH[tile] + TR)
                    last = nc.tensor.matmul(
                        o[:, rows, patch, :], turned[n % 2][0:IPIX, patch, tile, :],
                        band[0:IPIX, m, tile, :, patch * PC:(patch + 1) * PC],
                        start=tile == 0, stop=tile == TILED - 1, skip_group_check=True)
            last.then_inc(blended, 1)

        def strip(img, s, first, last):
            for c in range(CH):
                for m in range(PAIRS):
                    if first and c == 0 and m + 2 < PAIRS:
                        spread(img, s, m + 2)
                    if m + 1 < PAIRS:
                        cross(img, s, c, m + 1)
                    elif c + 1 < CH:
                        cross(img, s, c + 1, 0)
                    elif not last:
                        cross(img, s + 1, 0, 0)
                    multiply(img, s, c, m)
                    if c == CH - 1 and not last:
                        if m == 0:
                            pe.wait_ge(kw_in, 16 * (img * STRIPS + s + 2))
                        spread(img, s + 1, m)

        def blend(img, last):
            scans = img + 1 if last else img + 2
            pe.wait_ge(mapped, 2 * scans * UNITS + 1)
            pe.wait_ge(spread_ready, 2)
            cross(img, 0, 0, 0)
            pe.wait_ge(kw_in, 16 * (img * STRIPS + 1))
            for m in range(2):
                spread(img, 0, m)
            strip(img, 0, True, False)
            with pe.Fori(1, STRIPS - 1) as s:
                strip(img, s, False, False)
            strip(img, STRIPS - 1, False, True)

        pe.wait_ge(const_in, 64)
        for c in range(CH):
            last = nc.tensor.matmul(banks[7][:, c * TAPS:(c + 1) * TAPS], comp_sb[:, c * P:(c + 1) * P],
                                    gen_sb[:], start=True, stop=True, skip_group_check=True)
        last.then_inc(taps_made, 1)
        pe.wait_ge(taps_copied, 1)
        pe.wait_ge(spread_ready, 1)
        schedule(pe, scan, blend)

    @block.scalar
    def _(act):
        def exponent(img, u):
            act.wait_ge(centered, img * UNITS + u + 1)
            nc.scalar.activation(logits[:], logits[:], ACT.Exp).then_inc(powered, 1)

        def map_out(img, u):
            n = img * UNITS + u
            act.wait_ge(flipped, n + 2)
            act.wait_ge(planes_stored, 48 * n + 16)
            nc.scalar.copy(map_rows[:, 0:2, :], map_ps[0][0:K * UNIT_ROWS, :].rearrange(
                "p (g w) -> p g w", g=2)).then_inc(mapped, 1)
            nc.scalar.copy(map_rows[:, 2, :], map_ps[1][0:K * UNIT_ROWS, 0:W]).then_inc(mapped, 1)
            act.wait_ge(mapped, 2 * n + 3)
            dst = planes[bass.ds(img, 1)].rearrange("n k h w -> (n k) h w")
            for g in range(K):
                act.dma_start(dst[g * K:(g + 1) * K, bass.ds(u * UNIT_ROWS, UNIT_ROWS), :],
                              map_rows[:, g, :]).then_inc(planes_stored, 16)

        def scan(img):
            with act.Fori(0, UNITS) as u:
                exponent(img, u)
                map_out(img, u)

        def collect(img, s, m):
            act.wait_ge(blended, pairs(img, s, 1, m + 1))
            if m == 0:
                act.wait_ge(stored[1], 16 * (img * STRIPS + s + 1))
            nc.scalar.copy(out_rows[1][:, :, m * PAIR_COLS:(m + 1) * PAIR_COLS],
                           blend_ps[(PAIRS + m) % 2][:, 0:SR * PAIR_COLS].rearrange(
                               "p (y z) -> p y z", y=SR)).then_inc(collected_act, 1)

        def strip(img, s):
            for c in range(CH):
                for m in range(PAIRS):
                    n = c * PAIRS + m
                    act.wait_ge(crossed, pairs(img, s, c, m + 1))
                    act.wait_ge(blended, pairs(img, s, c, m - 1))
                    nc.scalar.copy(turned[n % 2][0:IPIX].rearrange("p a b c -> p (a b c)"),
                                   turn_ps[n % 2][0:IPIX, :]).then_inc(copied, 1)
                    if c == 1 and m:
                        collect(img, s, m - 1)

        def blend(img, last):
            with act.Fori(0, STRIPS) as s:
                strip(img, s)

        schedule(act, scan, blend)

    @block.vector
    def _(dve):
        def take_logits(img, u):
            n = img * UNITS + u
            dve.wait_ge(shifted, n + 2)
            for wh in range(WH):
                nc.vector.tensor_tensor(
                    logits[:, wh * UNIT_ROWS:(wh + 1) * UNIT_ROWS, :],
                    logit_ps[wh][:, 0:UNIT_ROWS * KK].rearrange("p (y k) -> p y k", k=KK),
                    rowsum[:, wh, :, KK:2 * KK], ALU.add).then_inc(logits_taken, 1)
            dve.wait_ge(logits_taken, 2 * n + 3)

        def softmax(img, u):
            n = img * UNITS + u
            bias = bias_sb[:].unsqueeze(1).to_broadcast((P, WH * UNIT_ROWS, KK))
            nc.vector.tensor_tensor(logits[:], logits[:], bias, ALU.add).then_inc(biased, 1)
            dve.wait_ge(biased, n + 1)
            nc.vector.reduce_max(top[:], logits[:], AX.X).then_inc(topped, 1)
            dve.wait_ge(topped, n + 1)

            def per_pixel(a):
                return a[:].unsqueeze(2).to_broadcast((P, WH * UNIT_ROWS, KK))
            nc.vector.tensor_tensor(logits[:], logits[:], per_pixel(top), ALU.subtract).then_inc(centered, 1)
            dve.wait_ge(powered, n + 1)
            nc.vector.reduce_sum(total[:], logits[:], AX.X).then_inc(totalled, 1)
            dve.wait_ge(totalled, n + 1)
            nc.vector.reciprocal(scale[:], total[:]).then_inc(inverted, 1)
            dve.wait_ge(inverted, n + 1)
            dve.wait_ge(flipped, n + 1)
            for wh in range(WH):
                rows = slice(wh * UNIT_ROWS, (wh + 1) * UNIT_ROWS)
                last = nc.vector.tensor_tensor(
                    probs[:, wh].rearrange("p k y -> p y k"), logits[:, rows, :],
                    scale[:, rows].unsqueeze(2).to_broadcast((P, UNIT_ROWS, KK)), ALU.mult)
            last.then_inc(probs_made, 1)

        def close_row(img, b, par):
            dve.wait_ge(lifted, img * BLOCKS + b)
            row = (par + 1) % 2 * BLOCK_ROWS + BLOCK_ROWS - 1
            for wh in range(WH):
                sums = rowsum[:, wh, row, :]
                last = nc.vector.tensor_tensor(sums, gather_ps[par][wh][:, 0:JK], sums, ALU.add)
            return last

        def lift(par, first=False):
            for wh in range(WH):
                ps = gather_ps[par][wh]
                rows = rowsum[:, wh, par * BLOCK_ROWS:(par + 1) * BLOCK_ROWS, :].rearrange("p y t -> p (y t)")
                at = 0
                if not first:
                    nc.vector.tensor_tensor(rows[:, 0:JK], ps[:, JK:2 * JK], carry[1 - par][:, wh], ALU.add)
                    at = JK
                nc.vector.tensor_copy(rows[:, at:], ps[:, JK + at:(BLOCK_ROWS + 1) * JK])
                last = nc.vector.tensor_copy(carry[par][:, wh], ps[:, (BLOCK_ROWS + 1) * JK:SLOTS_OF_SUMS * JK])
            last.then_inc(lifted, 1)

        def scan(img):
            dve.wait_ge(scanned, img * TILES + 2)
            lift(0, True)
            dve.wait_ge(scanned, img * TILES + SLOTS)
            close_row(img, 1, 1)
            lift(1)
            with dve.Fori(1, UNITS) as it:
                dve.wait_ge(scanned, img * TILES + it * SLOTS + 2)
                close_row(img, 2 * it, 0).then_inc(summed, 1)
                take_logits(img, it - 1)
                lift(0)
                softmax(img, it - 1)
                dve.wait_ge(scanned, img * TILES + (it + 1) * SLOTS)
                close_row(img, 2 * it + 1, 1)
                lift(1)
            take_logits(img, UNITS - 1)
            softmax(img, UNITS - 1)

        def matrices(img, s, m):
            dve.wait_ge(spreaded, bands(img, s, m + 1))
            dve.wait_ge(blended, pairs(img, s - 1, 1, m + 1))
            nc.vector.tensor_tensor(
                band[0:IPIX, m].rearrange("p t y z -> p (t y z)"),
                spread_ps[m % 2][0:IPIX, 0:TILED * TR * PAIR_COLS], mask[0:IPIX], ALU.mult).then_inc(banded, 1)

        def collect(img, s, c, m, signal):
            dve.wait_ge(blended, pairs(img, s, c, m + 1))
            if m == 0:
                dve.wait_ge(stored[c], 16 * (img * STRIPS + s + 1))
            cols = PAIR_COLS if m < PAIRS - 1 else LAST_COLS
            nc.vector.tensor_copy(
                out_rows[c][:, :, m * PAIR_COLS:m * PAIR_COLS + cols],
                blend_ps[(c * PAIRS + m) % 2][:, 0:SR * PAIR_COLS].rearrange(
                    "p (y z) -> p y z", y=SR)[:, :, 0:cols]).then_inc(signal, 1)

        INNER = (PATCHES - 2) // 4

        def lay_inner(src, c, to, n):
            rows = src.shape[1]
            inner = src[:, :, PC - 1:]
            nc.vector.tensor_copy(
                patches[c][:, 1 + n * INNER:1 + (n + 1) * INNER, to * IC:(to + rows) * IC].rearrange(
                    "p q (r s) -> p q r s", r=rows),
                bass.AP(inner.tensor, inner.offset + n * INNER * PC, [inner.ap[0], [PC, INNER], [W, rows], [1, IC]]))

        def lay_outer(src, c, to):
            rows = src.shape[1]
            dst = patches[c][:, :, to * IC:(to + rows) * IC].rearrange("p q (r s) -> p q r s", r=rows)
            right = (PATCHES - 1) * PC - 1
            nc.vector.tensor_copy(dst[:, 0, :, 1:IC], src[:, :, 0:IC - 1])
            nc.vector.tensor_copy(dst[:, PATCHES - 1, :, 0:W - right], src[:, :, right:W])
            for col, at, patch in ((1, 0, 0), (W - 2, W - right, PATCHES - 1)):
                last = nc.vector.tensor_copy(dst[:, patch, :, at], src[:, :, col])
            return last

        def lay_rows(src, c, to):
            for n in range(4):
                lay_inner(src, c, to, n)
            return lay_outer(src, c, to)

        def lay_part(img, s, c, part):
            if part == 0:
                dve.wait_ge(crossed, pairs(img, s - 1, c + 1))
                nc.vector.tensor_copy(patches[c][:, :, 0:2 * IC],
                                      patches[c][:, :, SR * IC:IR * IC]).then_inc(haloed, 1)
            if part == 1:
                dve.wait_ge(haloed, img * ((STRIPS - 1) * CH) + (s - 1) * CH + c + 1)
                dve.wait_ge(x_in[c], 32 * (img * STRIPS + s + 1))
            if 0 < part < 5:
                lay_inner(halves[c], c, 2, part - 1)
            if part == 5:
                lay_outer(halves[c], c, 2).then_inc(laid, 1)

        def lay_first(img, c):
            dve.wait_ge(crossed, pairs(img, 0))
            dve.wait_ge(x_in[c], 32 * (img * STRIPS + 1))
            dve.wait_ge(first_in, 16 * (img + 1))
            lay_rows(halves[c][:, 0:1], c, 0)
            lay_rows(first_row[:, c:c + 1], c, 1)
            nc.vector.memset(patches[c][:, PATCHES - 1].rearrange("p (r s) -> p r s", s=IC)[
                :, :, W - (PATCHES - 1) * PC + 2:], 0.0)
            lay_rows(halves[c], c, 2).then_inc(laid, 1)

        def blend(img, last):
            if not (last and images > 1):
                dve.wait_ge(scanned, (img + 1 if last else img + 2) * TILES)
            lay_first(img, 0)
            for m in range(2):
                matrices(img, 0, m)

            def strip(s, first, last):
                for m in range(PAIRS):
                    if first and m + 2 < PAIRS:
                        matrices(img, s, m + 2)
                    collect(img, s, 0, m, collected)
                    if first:
                        if m == 0:
                            lay_first(img, 1)
                    else:
                        lay_part(img, s, 1, m)
                for m in range(0 if last else PAIRS):
                    matrices(img, s + 1, m)
                    lay_part(img, s + 1, 0, m)
                collect(img, s, 1, PAIRS - 1, collected_last)

            strip(0, True, False)
            with dve.Fori(1, STRIPS - 1) as s:
                strip(s, False, False)
            strip(STRIPS - 1, False, True)

        nc.vector.memset(taps_sb[:, :, TAPS:], 0.0).then_inc(spread_ready, 1)
        dve.wait_ge(const_in, 64)
        nc.vector.tensor_copy(spread_sb[:].rearrange("p a b -> p (a b)"), spread32).then_inc(spread_ready, 1)
        dve.wait_ge(taps_made, 1)
        nc.vector.tensor_copy(taps_sb[:, :, 0:TAPS],
                              banks[7][:, 0:CH * TAPS].rearrange("p (c t) -> p c t", c=CH)).then_inc(taps_copied, 1)
        for at, (signal, n) in enumerate((
                (shifted, 1), (logits_taken, 1), (flipped, 1), (mapped, 1), (planes_stored, 16),
                (stored[0], 16), (stored[1], 16), (crossed, PAIR_COUNT), (copied, PAIR_COUNT),
                (blended, PAIR_COUNT), (spreaded, BAND_COUNT), (banded, BAND_COUNT), (collected, BAND_COUNT),
                (collected_act, STRIPS * (PAIRS - 1)), (collected_last, STRIPS), (laid, UNIT_COUNT))):
            nc.vector.memset(primer[:, at:at + 1], 0.0).then_inc(signal, n)
        schedule(dve, scan, blend)

    @block.gpsimd
    def _(pool):
        STEPS_A_CHUNK = 17

        def number(name, n=CHUNK):
            at = NUMBERS.index(name)
            return numbers[:, at:at + 1].to_broadcast((P, n))


        def chunk(img, ht, wc):
            n = img * CHUNKS + ht * (W // CHUNK) + wc
            count = n * STEPS_A_CHUNK
            done = 0

            def step(instruction):
                nonlocal done
                done += 1
                instruction.then_inc(refining, 1)
                pool.wait_ge(refining, count + done)

            w0 = wc * CHUNK
            nc.gpsimd.dma_start(raw[:].rearrange("p w k -> p (w k)"),
                                reread[bass.ds(img, 1)].rearrange("n h q -> (n h) q")[
                                    ht * P:(ht + 1) * P, w0 * KK:(w0 + CHUNK) * KK]).then_inc(raw_in, 16)
            pool.wait_ge(raw_in, 16 * (n + 1))
            for phase in range(K):
                first = (phase - w0) % K
                cols = slice(first, CHUNK, K)
                count_w = len(range(first, CHUNK, K))
                for j in range(K):
                    plane = (j + phase) % K
                    last = nc.gpsimd.tensor_tensor(
                        weighed[:, plane::K, cols],
                        raw[:, cols, j::K].rearrange("p w i -> p i w"),
                        window[:, :, j:j + 1].to_broadcast((P, K, count_w)), ALU.mult)
            step(last)
            sum4 = coef[:, 0:4]
            step(nc.gpsimd.tensor_tensor(sum4, weighed[:, 0:4], weighed[:, 4:8], ALU.add))
            sum2 = coef[:, 4:6]
            step(nc.gpsimd.tensor_tensor(sum2, sum4[:, 0:2], sum4[:, 2:4], ALU.add))
            step(nc.gpsimd.tensor_tensor(norm[:, 0], sum2[:, 0], sum2[:, 1], ALU.add))
            step(nc.gpsimd.tensor_tensor(norm[:, 1], norm[:, 0], weighed[:, 8], ALU.add))
            step(nc.gpsimd.tensor_tensor(norm[:, 0], norm[:, 1], number("eps"), ALU.add))
            step(nc.gpsimd.tensor_tensor(norm[:, 1], norm[:, 0], number("-1"), ALU.pow))
            step(nc.gpsimd.tensor_tensor(norm[:, 2], norm[:, 0], norm[:, 1], ALU.mult))
            step(nc.gpsimd.tensor_tensor(norm[:, 3], norm[:, 2], number("-2"), ALU.add))
            step(nc.gpsimd.tensor_tensor(norm[:, 0], norm[:, 1], norm[:, 3], ALU.mult))
            step(nc.gpsimd.tensor_tensor(coef[:], weighed[:], norm[:, 0:1].to_broadcast((P, KK, CHUNK)), ALU.mult))
            for phase in range(K):
                first = (phase - w0) % K
                centre = K + (1 + phase) % K
                mine = coef[:, centre, first::K]
                last = nc.gpsimd.tensor_tensor(mine, mine, number("2", mine.shape[1]), ALU.add)
            step(last)
            if ht or wc:
                pool.wait_ge(coefs_stored, 16 * n)
            high, mid, low = (pieces[:, part * KK:(part + 1) * KK] for part in range(PARTS))
            nothing = number("0").unsqueeze(1).to_broadcast((P, KK, CHUNK))
            step(nc.gpsimd.tensor_tensor(high, coef[:], nothing, ALU.add))
            step(nc.gpsimd.tensor_tensor(weighed[:], coef[:], high, ALU.subtract))
            step(nc.gpsimd.tensor_tensor(mid, weighed[:], nothing, ALU.add))
            step(nc.gpsimd.tensor_tensor(coef[:], weighed[:], mid, ALU.subtract))
            step(nc.gpsimd.tensor_tensor(low, coef[:], nothing, ALU.add))
            assert done == STEPS_A_CHUNK, done
            nc.gpsimd.dma_start(
                coefs[bass.ds(img, 1)].rearrange("n q h w -> h (n q) w")[ht * P:(ht + 1) * P, :, w0:w0 + CHUNK],
                pieces[:]).then_inc(coefs_stored, 16)

        nc.gpsimd.memset(kw[:], 0.0).then_inc(cleared, 1)
        pool.wait_ge(const_in, 64)
        with pool.Fori(0, images) as img:
            for ht in range(H // P):
                for wc in range(W // CHUNK):
                    if ht == 0 and wc == 0:
                        pool.wait_ge(planes_stored, 48 * UNITS * (img + 1) + 16)
                    chunk(img, ht, wc)
            pool.wait_ge(coefs_stored, 16 * CHUNKS * (img + 1))


_INS = ["x", "w_comp", "w_gen", "b_gen", "const"]


def program(nc, shapes):
    from contextlib import ExitStack
    f32 = mybir.dt.float32
    args = {n: nc.dram_tensor(n, shapes[n], f32, kind="ExternalInput").ap() for n in _INS}
    out = nc.dram_tensor("out", shapes["x"], f32, kind="ExternalOutput").ap()
    with ExitStack() as ctx:
        build(nc, ctx, *(args[n] for n in _INS), out, images=shapes["x"][0])


def kernel(x, L0_conv_w_comp, L0_conv_w_gen, L0_conv_b_gen):
    import concourse.bacc as bacc
    from concourse.bass_utils import run_bass_kernel_spmd

    gen = np.asarray(L0_conv_w_gen).transpose(1, 2, 3, 0)[:, ::-1].reshape(COMP, TAPS)
    arrays = {
        "x": np.ascontiguousarray(x),
        "w_comp": np.ascontiguousarray(L0_conv_w_comp),
        "w_gen": np.ascontiguousarray(gen),
        "b_gen": np.ascontiguousarray(L0_conv_b_gen).reshape(1, KK),
        "const": constants(),
    }
    nc = bacc.Bacc("TRN2", target_bir_lowering=False, num_devices=1)
    program(nc, {n: a.shape for n, a in arrays.items()})
    result = run_bass_kernel_spmd(nc, [arrays], core_ids=[0])
    return result.results[0]["out"]
```

```python
import numpy as np

import concourse.bass as bass
import concourse.mybir as mybir
from concourse.alu_op_type import AluOpType as ALU

B, C, H, W = 4, 256, 256, 256
COMP = 64
K = 3
KK = K * K
P = 128
CH = C // P
WH = W // P

TILE_ROWS = 8
SLOTS = 4
UNIT_ROWS = TILE_ROWS * SLOTS
UNITS = H // UNIT_ROWS
TILES = H // TILE_ROWS
BLOCK_ROWS = 16
BLOCKS = H // BLOCK_ROWS
SLOTS_OF_SUMS = BLOCK_ROWS + 2
JK = K * KK
TAPS = K * JK
TAP_COLS = 512 - (BLOCK_ROWS - 1) * JK & ~1

CHUNK = 128
CHUNKS = (H // P) * (W // CHUNK)

SR, PC = 16, 12
TR = 9
IC = PC + 2
IPIX = TR * IC
TILED = 2
REACH = [0, SR - TR]
IR = TILED * TR
STRIPS = H // SR
PATCHES = -(-W // PC)
PAIRS = PATCHES // 2
PAIR_COLS = 2 * PC
LAST_COLS = W - (PAIRS - 1) * PAIR_COLS
KW_PITCH = PATCHES * PC
PARTS = 3

UNIT_COUNT = STRIPS * CH
PAIR_COUNT = UNIT_COUNT * PAIRS
BAND_COUNT = STRIPS * PAIRS
assert STRIPS * SR == H and IR == SR + 2 and IPIX <= P and CH == 2 and PAIRS % 2 == 1
assert TILED * TR * PAIR_COLS <= 512 and SLOTS_OF_SUMS * JK <= 512


NUMBERS = ["eps", "-2", "-1", "0", "2"]


def constants():
    ident = np.eye(P)
    from_left = np.eye(P, k=1)
    from_right = np.eye(P, k=-1)
    spread = np.zeros((P, K, P))
    mask = np.zeros((P, TILED, TR, 2, PC))
    for r in range(TR):
        for s in range(IC):
            for phase in range(K):
                for part in range(PARTS):
                    spread[part * KK + (r - phase) % K * K + s % K, phase, r * IC + s] = 1
            for tile in range(TILED):
                for y in range(TR):
                    for z in range(PC):
                        i = tile * TR + r - REACH[tile] - y
                        mask[r * IC + s, tile, y, :, z] = 0 <= i < K and 0 <= s - z < K
    window = np.broadcast_to(np.outer(np.hamming(K), np.hamming(K)).reshape(-1), (P, KK))
    values = np.broadcast_to([1e-8 if n == "eps" else float(n) for n in NUMBERS], (P, len(NUMBERS)))
    return np.concatenate([ident, from_left, from_right,
                           spread.reshape(P, -1), mask.reshape(P, -1), window, values],
                          1).astype(np.float32)


def build(nc, ctx, x, w_comp, w_gen, b_gen, const, out, images=B):
    f32, bf16 = mybir.dt.float32, mybir.dt.bfloat16
    ACT = mybir.ActivationFunctionType
    AX = mybir.AxisListType

    def sb(name, shape, dt=f32):
        return ctx.enter_context(nc.sbuf_tensor(name, shape, dt))

    def sem(name):
        return ctx.enter_context(nc.semaphore(name))

    planes = nc.dram_tensor("planes", (images, KK, H, W), f32).ap()
    coefs = nc.dram_tensor("coefs", (images, PARTS * KK, H, W), bf16).ap()
    reread = planes.rearrange("n k h w -> n (k h w)").rearrange("n (h q) -> n h q", q=W * KK)

    x_rows = [sb(f"x_rows{c}", [P, CH * TILE_ROWS * W]) for c in range(CH)]
    patch_rows = [sb(f"patch_rows{c}", [P, PATCHES * IR * IC]) for c in range(CH)]
    tiles = [t[:, 0:CH * TILE_ROWS * W].rearrange("p (c h w) -> p c h w", c=CH, h=TILE_ROWS)
             for t in (*x_rows, *patch_rows)]
    halves = [t[:].rearrange("p (h w) -> p h w", h=SR) for t in x_rows]
    patches = [t[:].rearrange("p (q o) -> p q o", q=PATCHES) for t in patch_rows]
    first_row = sb("first_row", [P, CH, W])
    kw = sb("kw_strip", [P, SR, KW_PITCH], bf16)
    out_rows = [sb(f"out_rows{c}", [P, SR, W]) for c in range(CH)]
    const_sb = sb("const_sb", [P, const.shape[1]])
    spread_sb = sb("spread_sb", [P, K, P], bf16)
    comp_sb = sb("comp_sb", [COMP, C])
    gen_sb = sb("gen_sb", [COMP, TAPS])
    bias_sb = sb("bias_sb", [P, KK])
    taps_sb = sb("taps_sb", [P, CH, TAP_COLS])
    rowsum = sb("rowsum", [P, WH, UNIT_ROWS, JK])
    carry = [sb(f"carry{par}", [P, WH, JK]) for par in range(2)]
    logits = sb("logits", [P, WH * UNIT_ROWS, KK])
    top = sb("top", [P, WH * UNIT_ROWS])
    total = sb("total", [P, WH * UNIT_ROWS])
    scale = sb("scale", [P, WH * UNIT_ROWS])
    probs = sb("probs", [P, WH, KK, UNIT_ROWS])
    map_rows = sb("map_rows", [K * UNIT_ROWS, K, W])
    turned = [sb(f"turned{j}", [P, 2, TILED, P]) for j in range(2)]
    band = sb("band", [P, PAIRS, TILED, TR, PAIR_COLS])
    raw = sb("raw", [P, CHUNK, KK])
    weighed = sb("weighed", [P, KK, CHUNK])
    coef = sb("coef", [P, KK, CHUNK])
    pieces = sb("pieces", [P, PARTS * KK, CHUNK], bf16)
    norm = sb("norm", [P, 4, CHUNK])
    primer = sb("primer", [P, 32])

    at = 0
    def const_part(n):
        nonlocal at
        at += n
        return const_sb[:, at - n:at]
    ident, from_left, from_right = (const_part(P) for _ in range(3))
    spread32 = const_part(K * P)
    mask = const_part(TILED * TR * PAIR_COLS)
    window = const_part(KK).rearrange("p (i j) -> p i j", i=K)
    numbers = const_part(len(NUMBERS))

    banks = [ctx.enter_context(nc.psum_tensor(f"bank{n}", [P, 512], f32)) for n in range(8)]
    gather_ps = [[banks[2 * par + wh] for wh in range(WH)] for par in range(2)]
    logit_ps = banks[4:6]
    map_ps = banks[6:8]
    turn_ps = banks[0:2]
    spread_ps = banks[2:4]
    blend_ps = banks[4:6]

    weights_in = sem("weights_in")
    const_in = sem("const_in")
    cleared = sem("cleared")
    spread_ready = sem("spread_ready")
    taps_made = sem("taps_made")
    taps_copied = sem("taps_copied")
    tile_in = [sem(f"tile_in{q}") for q in range(SLOTS)]
    scanned = sem("scanned")
    summed = sem("summed")
    lifted = sem("lifted")
    shifted = sem("shifted")
    logits_taken = sem("logits_taken")
    summed_up = sem("summed_up")
    biased = sem("biased")
    topped = sem("topped")
    centered = sem("centered")
    powered = sem("powered")
    totalled = sem("totalled")
    inverted = sem("inverted")
    probs_made = sem("probs_made")
    flipped = sem("flipped")
    mapped = sem("mapped")
    planes_stored = sem("planes_stored")
    raw_in = sem("raw_in")
    refining = sem("refining")
    coefs_stored = sem("coefs_stored")
    first_in = sem("first_in")
    x_in = [sem(f"x_in{c}") for c in range(CH)]
    kw_in = sem("kw_in")
    haloed = sem("haloed")
    laid = sem("laid")
    crossed = sem("crossed")
    copied = sem("copied")
    spreaded = sem("spreaded")
    banded = sem("banded")
    blended = sem("blended")
    collected = sem("collected")
    collected_act = sem("collected_act")
    collected_last = sem("collected_last")
    stored = [sem(f"stored{c}") for c in range(CH)]

    def first_image(img):
        return isinstance(img, int) and img == 0

    def units(img, s, c=0):
        return (img + 1) * UNIT_COUNT + s * CH + c

    def pairs(img, s, c=0, m=0):
        return (img + 1) * PAIR_COUNT + s * (CH * PAIRS) + (c * PAIRS + m)

    def bands(img, s, m=0):
        return (img + 1) * BAND_COUNT + s * PAIRS + m

    def act_pairs(img, s, m=0):
        return (img + 1) * STRIPS * (PAIRS - 1) + s * (PAIRS - 1) + m

    def strips(img, s):
        return (img + 1) * STRIPS + s

    def ahead(eng, register, value):
        if isinstance(value, int):
            return value
        eng.reg_mov(register, value)
        return register

    block = ctx.enter_context(nc.Block())

    def schedule(eng, scan, blend):
        scan(0, "scan" if images > 1 else "blend")
        if images > 1:
            with eng.Fori(0, images - 2) as n:
                scan(n + 1, "blend")
                blend(n, "scan")
            scan(images - 1, "blend")
            blend(images - 2, "blend")
        blend(images - 1, None)

    def scans(img, nxt):
        return images if nxt is None else img + 2

    def to_finish(img, nxt):
        return None if nxt is None else img + 1

    @block.sync
    def _(sp):
        second_wait = sp.alloc_register("second_wait")

        def load_tile(img, it, q):
            src = x[bass.ds(img, 1)].rearrange("n (c p) h w -> p c (n h) w", c=CH)
            for c in range(CH):
                nc.sync.dma_start(tiles[q][:, c], src[:, c, bass.ds((it * SLOTS + q) * TILE_ROWS, TILE_ROWS), :])\
                    .then_inc(tile_in[q], 16)

        def enter_scan(img, q):
            if not first_image(img):
                if q < CH:
                    blend_through = ahead(sp, second_wait, units(img - 2, STRIPS - 1, q + 1))
                else:
                    blend_through = ahead(sp, second_wait, pairs(img - 2, STRIPS - 1, q + 1 - CH))
                sp.wait_ge(scanned, img * TILES - SLOTS + q + 1)
                sp.wait_ge(laid if q < CH else crossed, blend_through)
            load_tile(img, 0, q)

        def scan(img, nxt):
            with sp.Fori(1, UNITS) as it:
                for q in range(SLOTS):
                    sp.wait_ge(scanned, img * TILES + (it - 1) * SLOTS + q + 1)
                    load_tile(img, it, q)
            if nxt == "scan":
                for q in range(SLOTS):
                    enter_scan(img + 1, q)
            else:
                for c in range(CH):
                    sp.wait_ge(scanned, (img + 1) * TILES - SLOTS + c + 1)
                    enter_blend(img - 1 if images > 1 else img, c)
                first_kw(img - 1 if images > 1 else img)

        def load_half(img, s, c):
            src = x[bass.ds(img, 1)].rearrange("n (c p) h w -> p c (n h) w", c=CH)[:, c]
            rows = SR // 2
            for n in range(2):
                nc.sync.dma_start(halves[c][:, n * rows:(n + 1) * rows],
                                  src[:, bass.ds(s * SR + 1 + n * rows, rows), :]).then_inc(x_in[c], 16)

        def load_last_half(img, c):
            src = x[bass.ds(img, 1)].rearrange("n (c p) h w -> p c (n h) w", c=CH)[:, c]
            nc.sync.dma_start(halves[c][:, 0:SR - 1], src[:, H - SR + 1:H, :]).then_inc(x_in[c], 16)
            nc.sync.dma_start(halves[c][:, SR - 1], src[:, H - 2, :]).then_inc(x_in[c], 16)

        def load_kw(img, s):
            src = coefs[bass.ds(img, 1)].rearrange("n p h w -> p (n h) w")
            nc.sync.dma_start(kw[0:PARTS * KK, :, 0:W], src[:, bass.ds(s * SR, SR), :]).then_inc(kw_in, 16)

        def store(img, s, c):
            at = img * (C * H * W) + (s * (SR * W) + c * (P * H * W))
            dst = bass.AP(out.tensor, at, [[H * W, P], [1, SR * W]])
            if c == 0:
                sp.wait_ge(collected, bands(img, s + 1))
            else:
                last_done = ahead(sp, second_wait, strips(img, s + 1))
                sp.wait_ge(collected_act, act_pairs(img, s + 1))
                sp.wait_ge(collected_last, last_done)
            nc.sync.dma_start(dst, out_rows[c][:].rearrange("p y w -> p (y w)")).then_inc(stored[c], 16)

        def enter_blend(img, c):
            if c == 0:
                src = x[bass.ds(img, 1)].rearrange("n (c p) h w -> p c (n h) w", c=CH)
                nc.sync.dma_start(first_row[:], src[:, :, 0, :]).then_inc(first_in, 16)
            load_half(img, 0, c)

        def first_kw(img):
            sp.wait_ge(coefs_stored, 16 * CHUNKS * (img + 1))
            sp.wait_ge(cleared, 1)
            load_kw(img, 0)

        def load_next(img, s, load):
            for c in range(CH):
                sp.wait_ge(laid, units(img, s, c + 1))
                load(img, c)

        def strip(img, s):
            for c in range(CH):
                sp.wait_ge(laid, units(img, s, c + 1))
                load_half(img, s + 1, c)
                if isinstance(s, int) and c == 0:
                    sp.wait_ge(spreaded, bands(img, 1))
                    load_kw(img, 1)
            store(img, s, 0)
            sp.wait_ge(spreaded, bands(img, s + 2))
            load_kw(img, s + 2)
            store(img, s, 1)

        def blend(img, nxt):
            strip(img, 0)
            with sp.Fori(1, STRIPS - 2) as s:
                strip(img, s)
            s = STRIPS - 2
            load_next(img, s, load_last_half)
            store(img, s, 0)
            if nxt == "blend":
                sp.wait_ge(spreaded, bands(img, STRIPS))
                first_kw(img + 1)
            store(img, s, 1)
            s = STRIPS - 1
            if nxt == "scan":
                for q in range(SLOTS - 1):
                    enter_scan(img + 2, q)
            if nxt == "blend":
                load_next(img, s, lambda img, c: enter_blend(img + 1, c))
            store(img, s, 0)
            if nxt == "scan":
                enter_scan(img + 2, SLOTS - 1)
            store(img, s, 1)

        nc.sync.dma_start(comp_sb[:], w_comp).then_inc(weights_in, 16)
        nc.sync.dma_start(gen_sb[:], w_gen).then_inc(weights_in, 16)
        enter_scan(0, 0)
        nc.sync.dma_start(const_sb[:], const).then_inc(const_in, 16)
        nc.sync.dma_start(bias_sb[:], b_gen[0:1, :].to_broadcast((P, KK))).then_inc(const_in, 16)
        for q in range(1, SLOTS):
            enter_scan(0, q)
        schedule(sp, scan, blend)
        for slot in range(2):
            sp.wait_ge(stored[slot], 16 * (1 + images * STRIPS))

    @block.tensor
    def _(pe):
        def scan_row(img, rr, it):
            q, row = divmod(rr, TILE_ROWS)
            par, yy = divmod(rr, BLOCK_ROWS)
            if row == 0:
                pe.wait_ge(tile_in[q], 32 * (img * UNITS + it + 1))
            if yy == 0 and not isinstance(it, int):
                pe.wait_ge(lifted, img * BLOCKS + 2 * it + par - 1)
            for wh in range(WH):
                for c in range(CH):
                    last = nc.tensor.matmul(
                        gather_ps[par][wh][:, yy * JK:yy * JK + TAP_COLS],
                        tiles[q][:, c, row, wh::WH], taps_sb[:, c, :],
                        start=yy == 0 and c == 0, stop=yy == BLOCK_ROWS - 1 and c == CH - 1, skip_group_check=True)
            if row == TILE_ROWS - 1:
                last.then_inc(scanned, 1)

        def shift(img, u):
            pe.wait_ge(const_in, 32)
            if isinstance(u, int):
                pe.wait_ge(lifted, (img + 1) * BLOCKS)
            else:
                pe.wait_ge(summed, img * (UNITS - 1) + u + 1)
            pe.wait_ge(logits_taken, 2 * (img * UNITS + u) + 1)
            for even_or_odd, matrix, j in ((0, from_left, 0), (1, from_right, 2)):
                last = nc.tensor.matmul(logit_ps[even_or_odd][:, 0:UNIT_ROWS * KK], matrix,
                                        rowsum[:, 1 - even_or_odd, :, j * KK:(j + 1) * KK], start=True, stop=True)
            last.then_inc(shifted, 1)

        def flip(img, u):
            pe.wait_ge(probs_made, img * UNITS + u + 1)
            pe.wait_ge(mapped, 2 * (img * UNITS + u) + 1)
            for g in range(K):
                for wh in range(WH):
                    o = map_ps[g // 2][0:K * UNIT_ROWS, (g % 2) * W + wh * P:(g % 2) * W + (wh + 1) * P]
                    last = nc.tensor.transpose(
                        o, probs[:, wh, g * K:(g + 1) * K, :].rearrange("p k h -> p (k h)"), ident)
            last.then_inc(flipped, 1)

        def unit(img, it):
            for rr in range(UNIT_ROWS):
                scan_row(img, rr, it)
                if isinstance(it, int):
                    if rr == TILE_ROWS and not first_image(img):
                        pe.wait_ge(collected, bands(img - 2, STRIPS))
                        pe.wait_ge(collected_last, strips(img - 2, STRIPS))
                else:
                    if rr == BLOCK_ROWS + 3:
                        shift(img, it - 1)
                    if rr == UNIT_ROWS - 1:
                        flip(img, it - 1)

        def scan(img, nxt):
            if not first_image(img):
                pe.wait_ge(copied, pairs(img - 2, STRIPS))
                pe.wait_ge(banded, bands(img - 2, STRIPS))
                pe.wait_ge(lifted, img * BLOCKS)
            unit(img, 0)
            with pe.Fori(1, UNITS) as it:
                unit(img, it)
            if nxt == "scan" or images == 1:
                shift(img, UNITS - 1)
                flip(img, UNITS - 1)

        def cross(img, s, c, m):
            pe.wait_ge(copied, pairs(img, s, c, m - 1))
            if m == 0:
                pe.wait_ge(laid, units(img, s, c + 1))
            for patch in range(2):
                for tile in range(TILED):
                    at = (patch * TILED + tile) * P
                    last = nc.tensor.transpose(
                        turn_ps[(c * PAIRS + m) % 2][0:IPIX, at:at + P],
                        patches[c][:, 2 * m + patch, tile * IPIX:(tile + 1) * IPIX], ident)
            last.then_inc(crossed, 1)

        def spread(img, s, m):
            pe.wait_ge(banded, bands(img, s, m - 1 if m else 0))
            o = spread_ps[m % 2][:, 0:TILED * TR * PAIR_COLS].rearrange(
                "p (t y z) -> p t y z", t=TILED, y=TR)
            for phase in range(K):
                first = [next(y for y in range(r, SR) if y % K == phase) for r in REACH]
                stride = (first[1] - REACH[1] - first[0]) + TR
                src = bass.AP(kw, first[0] * KW_PITCH + m * PAIR_COLS,
                              [[SR * KW_PITCH, P], [(first[1] - first[0]) * KW_PITCH, TILED],
                               [K * KW_PITCH, TR // K], [1, PAIR_COLS]])
                dst = o[:, :, first[0]::K, :]
                dst = bass.AP(dst.tensor, dst.offset, [dst.ap[0], [stride * PAIR_COLS, TILED],
                                                       [K * PAIR_COLS, TR // K], [1, PAIR_COLS]])
                last = nc.tensor.matmul(dst, spread_sb[:, phase, :], src,
                                        start=True, stop=True, skip_group_check=True)
            last.then_inc(spreaded, 1)

        def multiply(img, s, c, m):
            pe.wait_ge(copied, pairs(img, s, c, m + 1))
            if c == 0:
                pe.wait_ge(banded, bands(img, s, m + 1))
            if m >= 2:
                if c == 0:
                    pe.wait_ge(collected, bands(img, s, m - 1))
                else:
                    pe.wait_ge(collected_act, act_pairs(img, s, m - 1))
            elif c == 1:
                pe.wait_ge(collected, bands(img, s, PAIRS - 1 + m))
            elif m == 0:
                pe.wait_ge(collected_act, act_pairs(img, s))
            else:
                pe.wait_ge(collected_last, strips(img, s))
            n = c * PAIRS + m
            o = blend_ps[n % 2][:, 0:SR * PAIR_COLS].rearrange("p (y q z) -> p y q z", y=SR, q=2)
            for patch in range(2):
                for tile in range(TILED):
                    rows = slice(REACH[tile], REACH[tile] + TR)
                    last = nc.tensor.matmul(
                        o[:, rows, patch, :], turned[n % 2][0:IPIX, patch, tile, :],
                        band[0:IPIX, m, tile, :, patch * PC:(patch + 1) * PC],
                        start=tile == 0, stop=tile == TILED - 1, skip_group_check=True)
            last.then_inc(blended, 1)

        def strip(img, s, first, last, finish=None):
            for c in range(CH):
                for m in range(PAIRS):
                    if first and c == 0 and m + 2 < PAIRS:
                        spread(img, s, m + 2)
                    if m + 1 < PAIRS:
                        cross(img, s, c, m + 1)
                    elif c + 1 < CH:
                        cross(img, s, c + 1, 0)
                    elif not last:
                        cross(img, s + 1, 0, 0)
                    multiply(img, s, c, m)
                    if finish is not None and c == 0 and m == PAIRS // 2:
                        flip(finish, UNITS - 1)
                    if c == CH - 1 and not last:
                        if m == 0:
                            pe.wait_ge(kw_in, 16 * (img * STRIPS + s + 2))
                        spread(img, s + 1, m)

        def blend(img, nxt):
            finish = to_finish(img, nxt)
            if finish is not None:
                pe.wait_ge(lifted, scans(img, nxt) * BLOCKS - 1)
            cross(img, 0, 0, 0)
            if finish is not None:
                shift(finish, UNITS - 1)
            pe.wait_ge(spread_ready, 2)
            pe.wait_ge(kw_in, 16 * (img * STRIPS + 1))
            for m in range(2):
                spread(img, 0, m)
            pe.wait_ge(logits_taken, 2 * (scans(img, nxt) * UNITS) + 1)
            strip(img, 0, True, False, finish)
            with pe.Fori(1, STRIPS - 1) as s:
                strip(img, s, False, False)
            strip(img, STRIPS - 1, False, True)

        pe.wait_ge(weights_in, 32)
        for c in range(CH):
            last = nc.tensor.matmul(banks[7][:, c * TAPS:(c + 1) * TAPS], comp_sb[:, c * P:(c + 1) * P],
                                    gen_sb[:], start=True, stop=True, skip_group_check=True)
        last.then_inc(taps_made, 1)
        pe.wait_ge(taps_copied, 1)
        pe.wait_ge(spread_ready, 1)
        schedule(pe, scan, blend)

    @block.scalar
    def _(act):
        def exponent(img, u):
            act.wait_ge(centered, img * UNITS + u + 1)
            nc.scalar.activation(logits[:], logits[:], ACT.Exp).then_inc(powered, 1)

        def map_out(img, u):
            n = img * UNITS + u
            act.wait_ge(flipped, n + 2)
            act.wait_ge(planes_stored, 48 * n + 16)
            nc.scalar.copy(map_rows[:, 0:2, :].rearrange("p g (w eo) -> p g eo w", eo=WH),
                           map_ps[0][0:K * UNIT_ROWS, :].rearrange(
                               "p (g eo w) -> p g eo w", g=2, eo=WH)).then_inc(mapped, 1)
            nc.scalar.copy(map_rows[:, 2, :].rearrange("p (w eo) -> p eo w", eo=WH),
                           map_ps[1][0:K * UNIT_ROWS, 0:W].rearrange("p (eo w) -> p eo w", eo=WH)).then_inc(mapped, 1)
            act.wait_ge(mapped, 2 * n + 3)
            dst = planes[bass.ds(img, 1)].rearrange("n k h w -> (n k) h w")
            for g in range(K):
                act.dma_start(dst[g * K:(g + 1) * K, bass.ds(u * UNIT_ROWS, UNIT_ROWS), :],
                              map_rows[:, g, :]).then_inc(planes_stored, 16)

        def scan(img, nxt):
            with act.Fori(0, UNITS if nxt == "scan" or images == 1 else UNITS - 1) as u:
                exponent(img, u)
                map_out(img, u)

        def collect(img, s, m):
            act.wait_ge(blended, pairs(img, s, 1, m + 1))
            if m == 0:
                act.wait_ge(stored[1], 16 * (img * STRIPS + s + 1))
            nc.scalar.copy(out_rows[1][:, :, m * PAIR_COLS:(m + 1) * PAIR_COLS],
                           blend_ps[(PAIRS + m) % 2][:, 0:SR * PAIR_COLS].rearrange(
                               "p (y z) -> p y z", y=SR)).then_inc(collected_act, 1)

        def strip(img, s, finish=None):
            for c in range(CH):
                for m in range(PAIRS):
                    if finish is not None and c == 0:
                        if m == 2:
                            exponent(finish, UNITS - 1)
                        if m == PAIRS - 2:
                            map_out(finish, UNITS - 1)
                    n = c * PAIRS + m
                    act.wait_ge(crossed, pairs(img, s, c, m + 1))
                    act.wait_ge(blended, pairs(img, s, c, m - 1))
                    nc.scalar.copy(turned[n % 2][0:IPIX].rearrange("p a b c -> p (a b c)"),
                                   turn_ps[n % 2][0:IPIX, :]).then_inc(copied, 1)
                    if c == 1 and m:
                        collect(img, s, m - 1)

        def blend(img, nxt):
            strip(img, 0, to_finish(img, nxt))
            with act.Fori(1, STRIPS) as s:
                strip(img, s)

        schedule(act, scan, blend)

    @block.vector
    def _(dve):
        def take_logits(img, u):
            n = img * UNITS + u
            dve.wait_ge(shifted, n + 2)
            for wh in range(WH):
                nc.vector.tensor_tensor(
                    logits[:, wh * UNIT_ROWS:(wh + 1) * UNIT_ROWS, :],
                    logit_ps[wh][:, 0:UNIT_ROWS * KK].rearrange("p (y k) -> p y k", k=KK),
                    rowsum[:, wh, :, KK:2 * KK], ALU.add).then_inc(logits_taken, 1)
            dve.wait_ge(logits_taken, 2 * n + 3)
            for even_or_odd, j in ((0, 2), (1, 0)):
                mine = logits[:, even_or_odd * UNIT_ROWS:(even_or_odd + 1) * UNIT_ROWS, :]
                last = nc.vector.tensor_tensor(
                    mine, mine, rowsum[:, 1 - even_or_odd, :, j * KK:(j + 1) * KK], ALU.add)
            last.then_inc(summed_up, 1)
            dve.wait_ge(summed_up, n + 1)

        def softmax(img, u, part):
            n = img * UNITS + u

            def per_pixel(a):
                return a[:].unsqueeze(2).to_broadcast((P, WH * UNIT_ROWS, KK))
            if part == 0:
                bias = bias_sb[:].unsqueeze(1).to_broadcast((P, WH * UNIT_ROWS, KK))
                nc.vector.tensor_tensor(logits[:], logits[:], bias, ALU.add).then_inc(biased, 1)
            if part == 1:
                dve.wait_ge(biased, n + 1)
                nc.vector.reduce_max(top[:], logits[:], AX.X).then_inc(topped, 1)
            if part == 2:
                dve.wait_ge(topped, n + 1)
                nc.vector.tensor_tensor(logits[:], logits[:], per_pixel(top), ALU.subtract).then_inc(centered, 1)
            if part == 3:
                dve.wait_ge(powered, n + 1)
                nc.vector.reduce_sum(total[:], logits[:], AX.X).then_inc(totalled, 1)
            if part == 4:
                dve.wait_ge(totalled, n + 1)
                nc.vector.reciprocal(scale[:], total[:]).then_inc(inverted, 1)
            if part == 5:
                dve.wait_ge(inverted, n + 1)
                dve.wait_ge(flipped, n + 1)
                for wh in range(WH):
                    rows = slice(wh * UNIT_ROWS, (wh + 1) * UNIT_ROWS)
                    last = nc.vector.tensor_tensor(
                        probs[:, wh].rearrange("p k y -> p y k"), logits[:, rows, :],
                        scale[:, rows].unsqueeze(2).to_broadcast((P, UNIT_ROWS, KK)), ALU.mult)
                last.then_inc(probs_made, 1)

        def close_row(img, b, par):
            dve.wait_ge(lifted, img * BLOCKS + b)
            row = (par + 1) % 2 * BLOCK_ROWS + BLOCK_ROWS - 1
            for wh in range(WH):
                sums = rowsum[:, wh, row, :]
                last = nc.vector.tensor_tensor(sums, gather_ps[par][wh][:, 0:JK], sums, ALU.add)
            return last

        def lift(par, first=False):
            for wh in range(WH):
                ps = gather_ps[par][wh]
                rows = rowsum[:, wh, par * BLOCK_ROWS:(par + 1) * BLOCK_ROWS, :].rearrange("p y t -> p (y t)")
                at = 0
                if not first:
                    nc.vector.tensor_tensor(rows[:, 0:JK], ps[:, JK:2 * JK], carry[1 - par][:, wh], ALU.add)
                    at = JK
                nc.vector.tensor_copy(rows[:, at:], ps[:, JK + at:(BLOCK_ROWS + 1) * JK])
                last = nc.vector.tensor_copy(carry[par][:, wh], ps[:, (BLOCK_ROWS + 1) * JK:SLOTS_OF_SUMS * JK])
            last.then_inc(lifted, 1)

        def scan(img, nxt):
            dve.wait_ge(scanned, img * TILES + 2)
            lift(0, True)
            dve.wait_ge(scanned, img * TILES + SLOTS)
            close_row(img, 1, 1)
            lift(1)

            def first_block(it):
                dve.wait_ge(scanned, img * TILES + it * SLOTS + 2)
                close_row(img, 2 * it, 0).then_inc(summed, 1)
                take_logits(img, it - 1)
                lift(0)
                for part in range(6):
                    softmax(img, it - 1, part)

            def second_block(it):
                dve.wait_ge(scanned, img * TILES + (it + 1) * SLOTS)
                close_row(img, 2 * it + 1, 1)
                lift(1)

            with dve.Fori(1, UNITS - 1) as it:
                first_block(it)
                second_block(it)
            first_block(UNITS - 1)
            if nxt == "blend":
                dve.wait_ge(scanned, (img + 1) * TILES - 1)
                for part in range(6):
                    lay_first(img - 1 if images > 1 else img, 0, part)
            second_block(UNITS - 1)
            take_logits(img, UNITS - 1)
            if nxt == "scan" or images == 1:
                for part in range(6):
                    softmax(img, UNITS - 1, part)

        def matrices(img, s, m):
            dve.wait_ge(spreaded, bands(img, s, m + 1))
            dve.wait_ge(blended, pairs(img, s - 1, 1, m + 1))
            nc.vector.tensor_tensor(
                band[0:IPIX, m].rearrange("p t y z -> p (t y z)"),
                spread_ps[m % 2][0:IPIX, 0:TILED * TR * PAIR_COLS], mask[0:IPIX], ALU.mult).then_inc(banded, 1)

        def collect(img, s, c, m, signal):
            dve.wait_ge(blended, pairs(img, s, c, m + 1))
            if m == 0:
                dve.wait_ge(stored[c], 16 * (img * STRIPS + s + 1))
            cols = PAIR_COLS if m < PAIRS - 1 else LAST_COLS
            nc.vector.tensor_copy(
                out_rows[c][:, :, m * PAIR_COLS:m * PAIR_COLS + cols],
                blend_ps[(c * PAIRS + m) % 2][:, 0:SR * PAIR_COLS].rearrange(
                    "p (y z) -> p y z", y=SR)[:, :, 0:cols]).then_inc(signal, 1)

        def lay_inner(src, c, to, n, pieces):
            rows = src.shape[1]
            inner = src[:, :, PC - 1:]
            count = (PATCHES - 2) // pieces
            nc.vector.tensor_copy(
                patches[c][:, 1 + n * count:1 + (n + 1) * count, to * IC:(to + rows) * IC].rearrange(
                    "p q (r s) -> p q r s", r=rows),
                bass.AP(inner.tensor, inner.offset + n * count * PC, [inner.ap[0], [PC, count], [W, rows], [1, IC]]))

        def lay_outer(src, c, to):
            rows = src.shape[1]
            dst = patches[c][:, :, to * IC:(to + rows) * IC].rearrange("p q (r s) -> p q r s", r=rows)
            right = (PATCHES - 1) * PC - 1
            nc.vector.tensor_copy(dst[:, 0, :, 1:IC], src[:, :, 0:IC - 1])
            nc.vector.tensor_copy(dst[:, PATCHES - 1, :, 0:W - right], src[:, :, right:W])
            for col, at, patch in ((1, 0, 0), (W - 2, W - right, PATCHES - 1)):
                last = nc.vector.tensor_copy(dst[:, patch, :, at], src[:, :, col])
            return last

        def lay_part(img, s, c, part):
            if part == 0:
                dve.wait_ge(crossed, pairs(img, s - 1, c + 1))
                nc.vector.tensor_copy(patches[c][:, :, 0:2 * IC],
                                      patches[c][:, :, SR * IC:IR * IC]).then_inc(haloed, 1)
            if part == 1:
                dve.wait_ge(haloed, img * ((STRIPS - 1) * CH) + (s - 1) * CH + c + 1)
                dve.wait_ge(x_in[c], 32 * (img * STRIPS + s + 1))
            if 0 < part < 5:
                lay_inner(halves[c], c, 2, part - 1, 4)
            if part == 5:
                lay_outer(halves[c], c, 2).then_inc(laid, 1)

        def lay_first(img, c, part):
            if part == 0:
                dve.wait_ge(first_in, 16 * (img + 1))
                dve.wait_ge(x_in[c], 32 * (img * STRIPS + 1))
                for src, to in ((halves[c][:, 0:1], 0), (first_row[:, c:c + 1], 1)):
                    lay_inner(src, c, to, 0, 1)
                    lay_outer(src, c, to)
            if 0 < part < 5:
                lay_inner(halves[c], c, 2, part - 1, 4)
            if part == 5:
                nc.vector.memset(patches[c][:, PATCHES - 1].rearrange("p (r s) -> p r s", s=IC)[
                    :, :, W - (PATCHES - 1) * PC + 2:], 0.0)
                lay_outer(halves[c], c, 2).then_inc(laid, 1)

        def first_strip(img, nxt):
            finish = to_finish(img, nxt)
            for m in range(2):
                if finish is not None:
                    softmax(finish, UNITS - 1, m)
                matrices(img, 0, m)
            for m in range(PAIRS):
                if finish is not None and m < 4:
                    softmax(finish, UNITS - 1, m + 2)
                if m + 2 < PAIRS:
                    matrices(img, 0, m + 2)
                collect(img, 0, 0, m, collected)
                if m == 3:
                    dve.wait_ge(scanned, scans(img, nxt) * TILES)
                    dve.wait_ge(crossed, pairs(img, 0))
                if m >= 3:
                    lay_first(img, 1, m - 3)
            for m in range(PAIRS):
                matrices(img, 1, m)
                lay_part(img, 1, 0, m)
            collect(img, 0, 1, PAIRS - 1, collected_last)

        def strip(img, s, nxt=None, last=False):
            for m in range(PAIRS):
                collect(img, s, 0, m, collected)
                lay_part(img, s, 1, m)
            for m in range(0 if last else PAIRS):
                matrices(img, s + 1, m)
                lay_part(img, s + 1, 0, m)
            if last and nxt == "blend":
                dve.wait_ge(crossed, pairs(img, s, 1))
                for part in range(6):
                    lay_first(img + 1, 0, part)
            collect(img, s, 1, PAIRS - 1, collected_last)

        def blend(img, nxt):
            first_strip(img, nxt)
            with dve.Fori(1, STRIPS - 1) as s:
                strip(img, s)
            strip(img, STRIPS - 1, nxt, True)

        nc.vector.memset(taps_sb[:, :, TAPS:], 0.0).then_inc(spread_ready, 1)
        dve.wait_ge(taps_made, 1)
        nc.vector.tensor_copy(taps_sb[:, :, 0:TAPS],
                              banks[7][:, 0:CH * TAPS].rearrange("p (c t) -> p c t", c=CH)).then_inc(taps_copied, 1)
        dve.wait_ge(const_in, 32)
        nc.vector.tensor_copy(spread_sb[:].rearrange("p a b -> p (a b)"), spread32).then_inc(spread_ready, 1)
        for at, (signal, n) in enumerate((
                (shifted, 1), (logits_taken, 1), (flipped, 1), (mapped, 1), (planes_stored, 16),
                (stored[0], 16), (stored[1], 16), (crossed, PAIR_COUNT), (copied, PAIR_COUNT),
                (blended, PAIR_COUNT), (spreaded, BAND_COUNT), (banded, BAND_COUNT), (collected, BAND_COUNT),
                (collected_act, STRIPS * (PAIRS - 1)), (collected_last, STRIPS), (laid, UNIT_COUNT))):
            nc.vector.memset(primer[:, at:at + 1], 0.0).then_inc(signal, n)
        schedule(dve, scan, blend)

    @block.gpsimd
    def _(pool):
        STEPS_A_CHUNK = 17

        def number(name, n=CHUNK):
            at = NUMBERS.index(name)
            return numbers[:, at:at + 1].to_broadcast((P, n))


        def chunk(img, ht, wc):
            n = img * CHUNKS + ht * (W // CHUNK) + wc
            count = n * STEPS_A_CHUNK
            done = 0

            def step(instruction):
                nonlocal done
                done += 1
                instruction.then_inc(refining, 1)
                pool.wait_ge(refining, count + done)

            w0 = wc * CHUNK
            nc.gpsimd.dma_start(raw[:].rearrange("p w k -> p (w k)"),
                                reread[bass.ds(img, 1)].rearrange("n h q -> (n h) q")[
                                    ht * P:(ht + 1) * P, w0 * KK:(w0 + CHUNK) * KK]).then_inc(raw_in, 16)
            pool.wait_ge(raw_in, 16 * (n + 1))
            for phase in range(K):
                first = (phase - w0) % K
                cols = slice(first, CHUNK, K)
                count_w = len(range(first, CHUNK, K))
                for j in range(K):
                    plane = (j + phase) % K
                    last = nc.gpsimd.tensor_tensor(
                        weighed[:, plane::K, cols],
                        raw[:, cols, j::K].rearrange("p w i -> p i w"),
                        window[:, :, j:j + 1].to_broadcast((P, K, count_w)), ALU.mult)
            step(last)
            sum4 = coef[:, 0:4]
            step(nc.gpsimd.tensor_tensor(sum4, weighed[:, 0:4], weighed[:, 4:8], ALU.add))
            sum2 = coef[:, 4:6]
            step(nc.gpsimd.tensor_tensor(sum2, sum4[:, 0:2], sum4[:, 2:4], ALU.add))
            step(nc.gpsimd.tensor_tensor(norm[:, 0], sum2[:, 0], sum2[:, 1], ALU.add))
            step(nc.gpsimd.tensor_tensor(norm[:, 1], norm[:, 0], weighed[:, 8], ALU.add))
            step(nc.gpsimd.tensor_tensor(norm[:, 0], norm[:, 1], number("eps"), ALU.add))
            step(nc.gpsimd.tensor_tensor(norm[:, 1], norm[:, 0], number("-1"), ALU.pow))
            step(nc.gpsimd.tensor_tensor(norm[:, 2], norm[:, 0], norm[:, 1], ALU.mult))
            step(nc.gpsimd.tensor_tensor(norm[:, 3], norm[:, 2], number("-2"), ALU.add))
            step(nc.gpsimd.tensor_tensor(norm[:, 0], norm[:, 1], norm[:, 3], ALU.mult))
            step(nc.gpsimd.tensor_tensor(coef[:], weighed[:], norm[:, 0:1].to_broadcast((P, KK, CHUNK)), ALU.mult))
            for phase in range(K):
                first = (phase - w0) % K
                centre = K + (1 + phase) % K
                mine = coef[:, centre, first::K]
                last = nc.gpsimd.tensor_tensor(mine, mine, number("2", mine.shape[1]), ALU.add)
            step(last)
            if ht or wc:
                pool.wait_ge(coefs_stored, 16 * n)
            high, mid, low = (pieces[:, part * KK:(part + 1) * KK] for part in range(PARTS))
            nothing = number("0").unsqueeze(1).to_broadcast((P, KK, CHUNK))
            step(nc.gpsimd.tensor_tensor(high, coef[:], nothing, ALU.add))
            step(nc.gpsimd.tensor_tensor(weighed[:], coef[:], high, ALU.subtract))
            step(nc.gpsimd.tensor_tensor(mid, weighed[:], nothing, ALU.add))
            step(nc.gpsimd.tensor_tensor(coef[:], weighed[:], mid, ALU.subtract))
            step(nc.gpsimd.tensor_tensor(low, coef[:], nothing, ALU.add))
            assert done == STEPS_A_CHUNK, done
            nc.gpsimd.dma_start(
                coefs[bass.ds(img, 1)].rearrange("n q h w -> h (n q) w")[ht * P:(ht + 1) * P, :, w0:w0 + CHUNK],
                pieces[:]).then_inc(coefs_stored, 16)

        nc.gpsimd.memset(kw[:], 0.0).then_inc(cleared, 1)
        pool.wait_ge(const_in, 32)
        with pool.Fori(0, images) as img:
            for ht in range(H // P):
                for wc in range(W // CHUNK):
                    if ht == 0 and wc == 0:
                        pool.wait_ge(planes_stored, 48 * UNITS * (img + 1) + 16)
                    chunk(img, ht, wc)
            pool.wait_ge(coefs_stored, 16 * CHUNKS * (img + 1))


_INS = ["x", "w_comp", "w_gen", "b_gen", "const"]


def program(nc, shapes):
    from contextlib import ExitStack
    f32 = mybir.dt.float32
    args = {n: nc.dram_tensor(n, shapes[n], f32, kind="ExternalInput").ap() for n in _INS}
    out = nc.dram_tensor("out", shapes["x"], f32, kind="ExternalOutput").ap()
    with ExitStack() as ctx:
        build(nc, ctx, *(args[n] for n in _INS), out, images=shapes["x"][0])


def kernel(x, L0_conv_w_comp, L0_conv_w_gen, L0_conv_b_gen):
    import concourse.bacc as bacc
    from concourse.bass_utils import run_bass_kernel_spmd

    gen = np.asarray(L0_conv_w_gen).transpose(1, 2, 3, 0)[:, ::-1].reshape(COMP, TAPS)
    arrays = {
        "x": np.ascontiguousarray(x),
        "w_comp": np.ascontiguousarray(L0_conv_w_comp),
        "w_gen": np.ascontiguousarray(gen),
        "b_gen": np.ascontiguousarray(L0_conv_b_gen).reshape(1, KK),
        "const": constants(),
    }
    nc = bacc.Bacc("TRN2", target_bir_lowering=False, num_devices=1)
    program(nc, {n: a.shape for n, a in arrays.items()})
    result = run_bass_kernel_spmd(nc, [arrays], core_ids=[0])
    return result.results[0]["out"]
```
